# Optimizing a Trainium2 kernel written in Bass

```python
import numpy as np
import jax
import jax.numpy as jnp

def _softmax(x, axis=-1):
    return jax.nn.softmax(x, axis=axis)

def _gelu(x):
    return jax.nn.gelu(x, approximate=True)

def _silu(x):
    return jax.nn.silu(x)

def _sigmoid(x):
    return jax.nn.sigmoid(x)

def _layernorm(x, axis=-1, eps=1e-05):
    m = jnp.mean(x, axis=axis, keepdims=True)
    v = jnp.var(x, axis=axis, keepdims=True)
    return (x - m) / jnp.sqrt(v + eps)

def _scatter_add(tgt, idx, src, axis=0):
    return tgt.at[idx].add(src)

def _segment_sum(src, seg, n):
    return jax.ops.segment_sum(src, seg, n)
kernel_name = 'mk_vit_tower_d1_tok_img1024_r4_e381e9'

def setup_inputs(seed: int=0):
    np.random.seed(seed)
    _w = jnp.asarray

    def _rec_inputs():
        import jax
        import jax.numpy as jnp
        _rk = jax.random.key(seed)
        x = -0.00016672 + 0.999947 * jax.random.normal(jax.random.fold_in(_rk, 1), (64, 3, 96, 96), jnp.float32)
        return x
    x = _rec_inputs()

    def _L0_tok_setup():
        import jax, jax.numpy as jnp
        import numpy as np
        EMBED_DIM = 256
        IMAGE_SIZE = 96
        CHANNELS = 3
        PATCH = 16
        NUM_PATCHES = (IMAGE_SIZE // PATCH) ** 2
        PATCH_DIM = PATCH * PATCH * CHANNELS

        def _patchify(x, patch):
            B, C, H, W = x.shape
            hp, wp = (H // patch, W // patch)
            x = x.reshape(B, C, hp, patch, wp, patch)
            x = x.transpose(0, 2, 4, 1, 3, 5)
            return x.reshape(B, hp * wp, C * patch * patch)
        key = jax.random.key(seed)
        k_x, k_w, k_b, k_cls, k_pos = jax.random.split(key, 5)
        x = jax.random.normal(k_x, (64, CHANNELS, IMAGE_SIZE, IMAGE_SIZE), dtype=jnp.float32)
        W = jax.random.normal(k_w, (EMBED_DIM, PATCH_DIM), dtype=jnp.float32) / np.sqrt(PATCH_DIM)
        b = jax.random.normal(k_b, (EMBED_DIM,), dtype=jnp.float32) * 0.01
        cls_token = jax.random.normal(k_cls, (1, 1, EMBED_DIM), dtype=jnp.float32)
        pos_embedding = jax.random.normal(k_pos, (1, 1 + NUM_PATCHES, EMBED_DIM), dtype=jnp.float32)
        return {'x': x, 'W': W, 'b': b, 'cls_token': cls_token, 'pos_embedding': pos_embedding}
    _L0_tok_all = _L0_tok_setup()
    _L0_tok_in = {k: v for k, v in _L0_tok_all.items() if k in ('W', 'b', 'cls_token', 'pos_embedding')}
    del _L0_tok_all

    def _L0_attn_setup():
        import math
        import jax, jax.numpy as jnp
        import numpy as np
        B, L, D_MODEL = (2, 512, 256)
        N_HEAD, HEAD_DIM = (16, 64)
        ATT_SCALE = 1.0
        key = jax.random.key(seed)
        ks = jax.random.split(key, 6)
        HD = N_HEAD * HEAD_DIM

        def xavier(k, fan_in, fan_out):
            lim = math.sqrt(6.0 / (fan_in + fan_out))
            return jax.random.uniform(k, (fan_in, fan_out), jnp.float32, -lim, lim)
        return {'x': jax.random.normal(ks[0], (B, L, D_MODEL), jnp.float32), 'Wq': xavier(ks[1], D_MODEL, HD), 'bq': jnp.zeros((HD,), jnp.float32), 'Wk': xavier(ks[2], D_MODEL, HD), 'bk': jnp.zeros((HD,), jnp.float32), 'Wv': xavier(ks[3], D_MODEL, HD), 'bv': jnp.zeros((HD,), jnp.float32), 'Wo': xavier(ks[4], HD, D_MODEL), 'bo': jax.random.uniform(ks[5], (D_MODEL,), jnp.float32, -1.0 / math.sqrt(HD), 1.0 / math.sqrt(HD))}
    _L0_attn_all = _L0_attn_setup()
    _L0_attn_in = {k: v for k, v in _L0_attn_all.items() if k in ('Wq', 'bq', 'Wk', 'bk', 'Wv', 'bv', 'Wo', 'bo')}
    del _L0_attn_all

    def _L0_ffn_setup():
        import jax, jax.numpy as jnp
        import numpy as np
        LATENT = 256
        LEAF_W = 64
        DEPTH = 4
        N_LEAVES = 2 ** DEPTH
        N_NODES = 2 ** DEPTH - 1
        B, S = (4, 512)

        def _fff_params(key, prefix):
            ks = jax.random.split(key, 4)
            d, h, l, n = (LATENT, LEAF_W, N_LEAVES, N_NODES)
            s_in = 1.0 / np.sqrt(d).astype(np.float32)
            s_h = 1.0 / np.sqrt(h).astype(np.float32)
            return {f'{prefix}_node_w': jax.random.normal(ks[0], (n, d), jnp.float32) * s_in, f'{prefix}_node_b': jax.random.normal(ks[1], (n,), jnp.float32) * s_in, f'{prefix}_w1': jax.random.normal(ks[2], (l, d, h), jnp.float32) * s_in, f'{prefix}_b1': jnp.zeros((l, h), jnp.float32), f'{prefix}_w2': jax.random.normal(ks[3], (l, h, d), jnp.float32) * s_h, f'{prefix}_b2': jnp.zeros((l, d), jnp.float32)}

        def _fff(x, node_w, node_b, w1, b1, w2, b2):
            Bx, Sx, D = x.shape
            xf = x.reshape(-1, D)
            N = xf.shape[0]
            cur = jnp.zeros((N,), jnp.int32)
            for _ in range(DEPTH):
                pw = node_w[cur]
                score = jnp.einsum('nd,nd->n', xf, pw) + node_b[cur]
                cur = 2 * cur + 1 + (score >= 0).astype(jnp.int32)
            leaf = cur - N_NODES
            sel = jax.nn.one_hot(leaf, N_LEAVES, dtype=xf.dtype)
            hidden_all = jax.nn.relu(jnp.einsum('nd,ldh->lnh', xf, w1) + b1[:, None, :])
            hidden = hidden_all * sel.T[:, :, None]
            out = jnp.einsum('lnh,lho->no', hidden, w2) + sel @ b2
            return out.reshape(Bx, Sx, D)
        key = jax.random.key(seed)
        kx, kq, kk, kv = jax.random.split(key, 4)
        inp = {'x': jax.random.normal(kx, (B, S, LATENT), jnp.float32)}
        inp.update(_fff_params(kq, 'q'))
        inp.update(_fff_params(kk, 'k'))
        inp.update(_fff_params(kv, 'v'))
        return inp
    _L0_ffn_all = _L0_ffn_setup()
    _L0_ffn_in = {k: v for k, v in _L0_ffn_all.items() if k in ('q_node_w', 'q_node_b', 'q_w1', 'q_b1', 'q_w2', 'q_b2', 'k_node_w', 'k_node_b', 'k_w1', 'k_b1', 'k_w2', 'k_b2', 'v_node_w', 'v_node_b', 'v_w1', 'v_b1', 'v_w2', 'v_b2')}
    del _L0_ffn_all
    return {'x': x, 'L0_tok_W': _L0_tok_in['W'], 'L0_tok_b': _L0_tok_in['b'], 'L0_tok_cls_token': _L0_tok_in['cls_token'], 'L0_tok_pos_embedding': _L0_tok_in['pos_embedding'], 'L0_attn_Wq': _L0_attn_in['Wq'], 'L0_attn_bq': _L0_attn_in['bq'], 'L0_attn_Wk': _L0_attn_in['Wk'], 'L0_attn_bk': _L0_attn_in['bk'], 'L0_attn_Wv': _L0_attn_in['Wv'], 'L0_attn_bv': _L0_attn_in['bv'], 'L0_attn_Wo': _L0_attn_in['Wo'], 'L0_attn_bo': _L0_attn_in['bo'], 'L0_ffn_q_node_w': _L0_ffn_in['q_node_w'], 'L0_ffn_q_node_b': _L0_ffn_in['q_node_b'], 'L0_ffn_q_w1': _L0_ffn_in['q_w1'], 'L0_ffn_q_b1': _L0_ffn_in['q_b1'], 'L0_ffn_q_w2': _L0_ffn_in['q_w2'], 'L0_ffn_q_b2': _L0_ffn_in['q_b2'], 'L0_ffn_k_node_w': _L0_ffn_in['k_node_w'], 'L0_ffn_k_node_b': _L0_ffn_in['k_node_b'], 'L0_ffn_k_w1': _L0_ffn_in['k_w1'], 'L0_ffn_k_b1': _L0_ffn_in['k_b1'], 'L0_ffn_k_w2': _L0_ffn_in['k_w2'], 'L0_ffn_k_b2': _L0_ffn_in['k_b2'], 'L0_ffn_v_node_w': _L0_ffn_in['v_node_w'], 'L0_ffn_v_node_b': _L0_ffn_in['v_node_b'], 'L0_ffn_v_w1': _L0_ffn_in['v_w1'], 'L0_ffn_v_b1': _L0_ffn_in['v_b1'], 'L0_ffn_v_w2': _L0_ffn_in['v_w2'], 'L0_ffn_v_b2': _L0_ffn_in['v_b2']}

def reference(x, L0_tok_W, L0_tok_b, L0_tok_cls_token, L0_tok_pos_embedding, L0_attn_Wq, L0_attn_bq, L0_attn_Wk, L0_attn_bk, L0_attn_Wv, L0_attn_bv, L0_attn_Wo, L0_attn_bo, L0_ffn_q_node_w, L0_ffn_q_node_b, L0_ffn_q_w1, L0_ffn_q_b1, L0_ffn_q_w2, L0_ffn_q_b2, L0_ffn_k_node_w, L0_ffn_k_node_b, L0_ffn_k_w1, L0_ffn_k_b1, L0_ffn_k_w2, L0_ffn_k_b2, L0_ffn_v_node_w, L0_ffn_v_node_b, L0_ffn_v_w1, L0_ffn_v_b1, L0_ffn_v_w2, L0_ffn_v_b2):
    import jax
    import jax.numpy as jnp

    def _L0_tok_ref(x, W, b, cls_token, pos_embedding):
        import jax, jax.numpy as jnp
        import numpy as np
        EMBED_DIM = 256
        IMAGE_SIZE = 96
        CHANNELS = 3
        PATCH = 16
        NUM_PATCHES = (IMAGE_SIZE // PATCH) ** 2
        PATCH_DIM = PATCH * PATCH * CHANNELS

        def _patchify(x, patch):
            B, C, H, W = x.shape
            hp, wp = (H // patch, W // patch)
            x = x.reshape(B, C, hp, patch, wp, patch)
            x = x.transpose(0, 2, 4, 1, 3, 5)
            return x.reshape(B, hp * wp, C * patch * patch)
        B = x.shape[0]
        patches = _patchify(x, PATCH)
        tokens = jnp.einsum('bnd,ed->bne', patches, W) + b
        cls = jnp.broadcast_to(cls_token, (B, 1, EMBED_DIM))
        out = jnp.concatenate([cls, tokens], axis=1)
        return out + pos_embedding

    def _L0_attn_ref(x, Wq, bq, Wk, bk, Wv, bv, Wo, bo):
        import math
        import jax, jax.numpy as jnp
        import numpy as np
        B, L, D_MODEL = (2, 512, 256)
        N_HEAD, HEAD_DIM = (16, 64)
        ATT_SCALE = 1.0
        b, l, _ = x.shape
        q = (x @ Wq + bq).reshape(b, l, N_HEAD, HEAD_DIM)
        k = (x @ Wk + bk).reshape(b, l, N_HEAD, HEAD_DIM)
        v = (x @ Wv + bv).reshape(b, l, N_HEAD, HEAD_DIM)
        scale = 1.0 / math.sqrt(HEAD_DIM ** ATT_SCALE)
        scores = jnp.einsum('blhd,bmhd->bhlm', q, k) * scale
        attn = jnp.einsum('bhlm,bmhd->blhd', scores, v)
        out = attn.reshape(b, l, N_HEAD * HEAD_DIM) @ Wo + bo
        return out

    def _L0_ffn_ref(x, q_node_w, q_node_b, q_w1, q_b1, q_w2, q_b2, k_node_w, k_node_b, k_w1, k_b1, k_w2, k_b2, v_node_w, v_node_b, v_w1, v_b1, v_w2, v_b2):
        import jax, jax.numpy as jnp
        import numpy as np
        LATENT = 256
        LEAF_W = 64
        DEPTH = 4
        N_LEAVES = 2 ** DEPTH
        N_NODES = 2 ** DEPTH - 1
        B, S = (4, 512)

        def _fff_params(key, prefix):
            ks = jax.random.split(key, 4)
            d, h, l, n = (LATENT, LEAF_W, N_LEAVES, N_NODES)
            s_in = 1.0 / np.sqrt(d).astype(np.float32)
            s_h = 1.0 / np.sqrt(h).astype(np.float32)
            return {f'{prefix}_node_w': jax.random.normal(ks[0], (n, d), jnp.float32) * s_in, f'{prefix}_node_b': jax.random.normal(ks[1], (n,), jnp.float32) * s_in, f'{prefix}_w1': jax.random.normal(ks[2], (l, d, h), jnp.float32) * s_in, f'{prefix}_b1': jnp.zeros((l, h), jnp.float32), f'{prefix}_w2': jax.random.normal(ks[3], (l, h, d), jnp.float32) * s_h, f'{prefix}_b2': jnp.zeros((l, d), jnp.float32)}

        def _fff(x, node_w, node_b, w1, b1, w2, b2):
            Bx, Sx, D = x.shape
            xf = x.reshape(-1, D)
            N = xf.shape[0]
            cur = jnp.zeros((N,), jnp.int32)
            for _ in range(DEPTH):
                pw = node_w[cur]
                score = jnp.einsum('nd,nd->n', xf, pw) + node_b[cur]
                cur = 2 * cur + 1 + (score >= 0).astype(jnp.int32)
            leaf = cur - N_NODES
            sel = jax.nn.one_hot(leaf, N_LEAVES, dtype=xf.dtype)
            hidden_all = jax.nn.relu(jnp.einsum('nd,ldh->lnh', xf, w1) + b1[:, None, :])
            hidden = hidden_all * sel.T[:, :, None]
            out = jnp.einsum('lnh,lho->no', hidden, w2) + sel @ b2
            return out.reshape(Bx, Sx, D)
        q = _fff(x, q_node_w, q_node_b, q_w1, q_b1, q_w2, q_b2)
        k = _fff(x, k_node_w, k_node_b, k_w1, k_b1, k_w2, k_b2)
        v = _fff(x, v_node_w, v_node_b, v_w1, v_b1, v_w2, v_b2)
        scale = 1.0 / np.sqrt(LATENT).astype(np.float32)
        attn = jax.nn.softmax(jnp.einsum('bqd,bkd->bqk', q, k) * scale, axis=-1)
        return jnp.einsum('bqk,bkd->bqd', attn, v)
    h = _L0_tok_ref(x, L0_tok_W, L0_tok_b, L0_tok_cls_token, L0_tok_pos_embedding)
    h = h + _L0_attn_ref(_layernorm(h, axis=-1), L0_attn_Wq, L0_attn_bq, L0_attn_Wk, L0_attn_bk, L0_attn_Wv, L0_attn_bv, L0_attn_Wo, L0_attn_bo)
    h = h + _L0_ffn_ref(_layernorm(h, axis=-1), L0_ffn_q_node_w, L0_ffn_q_node_b, L0_ffn_q_w1, L0_ffn_q_b1, L0_ffn_q_w2, L0_ffn_q_b2, L0_ffn_k_node_w, L0_ffn_k_node_b, L0_ffn_k_w1, L0_ffn_k_b1, L0_ffn_k_w2, L0_ffn_k_b2, L0_ffn_v_node_w, L0_ffn_v_node_b, L0_ffn_v_w1, L0_ffn_v_b1, L0_ffn_v_w2, L0_ffn_v_b2)
    return h

_drawn_inputs = setup_inputs


def setup_inputs(seed=0):
    import zlib

    import numpy as np

    out = dict(_drawn_inputs(seed))
    spreads = {'L0_attn_bq': (0.0, 0.1),
     'L0_attn_bk': (0.0, 0.1),
     'L0_attn_bv': (0.0, 0.1),
     'L0_ffn_q_b1': (0.0, 0.8),
     'L0_ffn_q_b2': (0.0, 0.8),
     'L0_ffn_k_b1': (0.0, 0.8),
     'L0_ffn_k_b2': (0.0, 0.8),
     'L0_ffn_v_b1': (0.0, 0.8),
     'L0_ffn_v_b2': (0.0, 0.67)}
    factors = {'L0_tok_b': 3.8,
     'L0_attn_bo': 6.078,
     'L0_ffn_q_node_b': 8.0,
     'L0_ffn_q_w1': 2.89,
     'L0_ffn_k_node_b': 8.0,
     'L0_ffn_k_w1': 2.836,
     'L0_ffn_v_node_b': 3.093}
    for name, (base, spread) in spreads.items():
        noise = np.random.default_rng([zlib.crc32(name.encode()), seed]).standard_normal(out[name].shape)
        drawn = base * np.exp(spread * noise) if base else spread * noise
        out[name] = jnp.asarray(drawn.astype(out[name].dtype))
    for name, factor in factors.items():
        out[name] = (out[name] * factor).astype(out[name].dtype)
    return out
```

```python
import concourse.bass as bass
from concourse import mybir
from contextlib import ExitStack
import numpy as np

IMAGES, CHANNELS, SIDE, PATCH, D = 64, 3, 96, 16, 256
PATCHES = (SIDE // PATCH) ** 2
PER_TILE = 3
ROWS = PER_TILE * (PATCHES + 1) + 1
TILES = -(-IMAGES // PER_TILE)
GT = 4
GROUPS = -(-TILES // GT)
TAIL = TILES - GT * (GROUPS - 1)
W = GT * ROWS
KX = CHANNELS * PATCH * PATCH // 128
KD = D // 128
HEADS, HD = 16, 64
PAIRS = HEADS // 2
INNER = HEADS * HD
TREES, LEAVES, NODES, LEAF_W, DEPTH = 3, 16, 15, 64, 4
HID = LEAVES * LEAF_W
CH = HID // 128
BIG = 2.0 ** 126
EPS = 1e-5

OFF_ROW = 0
ONE_ROW = 48
SEL_ROW = 64

XHI, XLO = 0, GT * KX * ROWS
WT = 2 * GT * KX * ROWS
WQ = WT + 2 * KX * D
WSIZE = 2 * KD * INNER
WK, WV, WO = WQ + WSIZE, WQ + 2 * WSIZE, WQ + 3 * WSIZE
ARENA = WO + WSIZE
W1 = [0, WQ, WV]
W2 = [WSIZE, WK, WO]

STAGE = 1024
NODE_W = -1
PIECES, _at = [], 0
for _dst, _n in [(WT, KX * D), (WV, WSIZE // 2), (WQ, WSIZE // 2), (WK, WSIZE // 2), (NODE_W, KD * 128),
                 (WO, WSIZE // 2)] + [(w, WSIZE // 2) for t in range(TREES) for w in (W1[t], W2[t])]:
    for _c in range(0, _n, STAGE):
        PIECES.append((_at + _c, min(STAGE, _n - _c), _dst, _n, _c))
    _at += _n
W_COLS = _at


def pieces_until(dst, last=False):
    found = [i for i, p in enumerate(PIECES) if p[2] == dst]
    if not last:
        first = found[0]
        found = [i for i in found if i - first < -(-PIECES[first][3] // STAGE)]
    return found[-1] + 1


P1_PIECES = pieces_until(WO)


CONSTS = 9


def first_group(g):
    return isinstance(g, int) and g == 0


def build_program(nc, x, weights, pos, tok, ident, mask, mask_bias, bv, bo, cols, e_mask, b1, b2, steer, out):
    f32, f32r, bf16 = mybir.dt.float32, mybir.dt.float32r, mybir.dt.bfloat16
    ALU, ACT, AX = mybir.AluOpType, mybir.ActivationFunctionType, mybir.AxisListType
    R = ROWS
    HW = GT * R // 2

    with ExitStack() as ctx:
        def sb(name, shape, dt=f32):
            return ctx.enter_context(nc.sbuf_tensor("sb_" + name, shape, dt))

        def sem(name):
            return ctx.enter_context(nc.semaphore(name))

        arena = sb("arena", [128, ARENA], f32r)
        node_w = sb("node_w", [128, 2, KD, 128], f32r)
        xT = sb("xT", [128, 2, KD, W], f32r)
        pairT = sb("pairT", [128, 3, 2, W], f32r)
        e_sb = sb("e_sb", [128, TREES, HID], bf16)
        b2_sb = sb("b2_sb", [128, 3, TREES, D], bf16)
        routeT = sb("routeT", [128, W], bf16)
        bitsT = sb("bitsT", [128, W], bf16)
        steer_sb = sb("steer_sb", [128, 128], bf16)
        x_raw = sb("x_raw", [128, GT, KX * R])
        stage = sb("stage", [128, 2, STAGE])
        h_all = sb("h_all", [128, TILES, D])
        xn = sb("xn", [R, GT, D])
        q_pad = sb("q_pad", [128, 2, GT, 2, R])
        k_sb = sb("k_sb", [128, 2, W])
        v_sb = sb("v_sb", [128, 2, GT, D])
        s_sb = sb("s_sb", [R, 2, GT, 2 * R])
        bv_sb = sb("bv_sb", [R, INNER])
        bo_sb = sb("bo_sb", [R, D])
        pos_sb = sb("pos_sb", [R, D])
        mask_sb = sb("mask_sb", [R, R])
        maskb_sb = sb("maskb_sb", [R, R])
        id_sb = sb("id_sb", [128, 128])
        cols_sb = sb("cols_sb", [128, 2 * PAIRS + 2])
        stats = sb("stats", [R, GT, 6])
        mv = sb("mv", [R, GT, 2])
        bearer = sb("bearer", [R, 2])
        std = sb("std", [R, GT])
        rstd = sb("rstd", [R, GT])
        mean2 = sb("mean2", [R, TILES])
        var2 = sb("var2", [R, TILES])
        std2 = sb("std2", [R, TILES])
        rstd2 = sb("rstd2", [R, TILES])
        neg_max = sb("neg_max", [R, GT])
        row_sum = sb("row_sum", [R, GT])
        row_inv = sb("row_inv", [R, GT])
        qT = q_pad[:, :, :, :, :].rearrange("p a t b r -> p (a t b r)").rearrange("p (z k w) -> p z k w", z=2, k=KD)
        soft_in = s_sb[:, 0, 0:2, :].rearrange("p a b -> p (a b)")
        probs = s_sb[:, 0, 2:4, :].rearrange("p a b -> p (a b)")
        probsT = s_sb[:, 1, 0:2, :].rearrange("p a b -> p (a b)")
        v2 = v_sb[0:R, 0, :, :]
        out_sb = v_sb[0:R, 1, :, :]

        banks = [ctx.enter_context(nc.psum_tensor(f"bank{i}", [128, 512], f32)) for i in range(8)]
        ring = banks[0:2]
        wo_acc = banks[2:4]
        s_ps = banks[4:6]
        o_ps = banks[6:8]
        hid_ps = banks[2:5]
        down = banks[5:7]

        consts = sem("consts")
        pos_ready = sem("pos_ready")
        bias_in = sem("bias_in")
        bias_step = sem("bias_step")
        bias_rows = sem("bias_rows")
        prelude = sem("prelude")
        x_loaded = sem("x_loaded")
        staged = [sem("staged0"), sem("staged1")]
        piece_hi = sem("piece_hi")
        piece_lo = sem("piece_lo")
        x_hi = sem("x_hi")
        x_lo = sem("x_lo")
        tok_done = sem("tok_done")
        h_ready = sem("h_ready")
        stat_step = sem("stat_step")
        var_ready = sem("var_ready")
        std_ready = sem("std_ready")
        xn_ready = sem("xn_ready")
        bo_added = sem("bo_added")
        centred = sem("centred")
        t_done = sem("t_done")
        xT_hi = sem("xT_hi")
        xT_lo = sem("xT_lo")
        v_done = sem("v_done")
        v_ready = sem("v_ready")
        q_done = sem("q_done")
        q_ready = sem("q_ready")
        k_done = sem("k_done")
        k_ready = sem("k_ready")
        s_done = sem("s_done")
        s_ready = sem("s_ready")
        o_done = sem("o_done")
        o_hi = sem("o_hi")
        o_lo = sem("o_lo")
        wo_done = sem("wo_done")
        h2_ready = sem("h2_ready")
        var2_ready = sem("var2_ready")
        std2_ready = sem("std2_ready")
        rstd2_ready = sem("rstd2_ready")
        score_done = sem("score_done")
        bits_ready = sem("bits_ready")
        count_done = sem("count_done")
        route_ready = sem("route_ready")
        up_done = sem("up_done")
        hid_hi = sem("hid_hi")
        hid_lo = sem("hid_lo")
        down_done = sem("down_done")
        down_q = sem("down_q")
        down_v = sem("down_v")
        att_done = sem("att_done")
        soft_step = sem("soft_step")
        max_ready = sem("max_ready")
        exp_ready = sem("exp_ready")
        pt_done = sem("pt_done")
        pt_ready = sem("pt_ready")
        av_done = sem("av_done")
        out_ready = sem("out_ready")
        stored = sem("stored")

        def part(base, size, low):
            return arena[:, base + low * size:base + (low + 1) * size]

        def tok_w(k, low):
            return part(WT, KX * D, low)[:, k * D:(k + 1) * D]

        def in_w(base, k, c, n, low):
            return part(base, KD * INNER, low)[:, k * INNER + c:k * INNER + c + n]

        def out_w(base, c, m, n, low):
            return part(base, CH * D, low)[:, c * D + m:c * D + m + n]

        def piece_dst(i, low):
            _, n, dst, size, off = PIECES[i]
            if dst == NODE_W:
                return node_w[:, low, :, :].rearrange("p k n -> p (k n)")
            return part(dst, size, low)[:, off:off + n]

        PRODUCTS = [(0, 0), (0, 1), (1, 0)]

        def tiles_of(g, lo, n):
            return bass.ds(g * GT + lo, n)

        def for_groups(eng, body):
            body(0, GT, GT)
            with eng.Fori(1, GROUPS - 2) as g:
                body(g, GT, GT)
            body(GROUPS - 2, GT, TAIL)
            body(GROUPS - 1, TAIL, 0)

        block = ctx.enter_context(nc.Block())

        @block.sync
        def _(sp):
            def load_x(g, nt):
                sp.dma_start(x_raw[:, 0:nt, :], x[tiles_of(g, 0, nt), :, :].rearrange("t p n -> p t n")).then_inc(x_loaded, 16)

            def load_piece(i):
                at, n, _, _, _ = PIECES[i]
                if i >= 2:
                    sp.wait_ge(piece_lo, i - 1)
                sp.dma_start(stage[:, i % 2, 0:n], weights[:, at:at + n]).then_inc(staged[i % 2], 16)

            load_piece(0)
            load_piece(1)
            load_x(0, GT)
            for dst, src in ((pos_sb, pos), (xn[:, 0, :], tok), (id_sb, ident), (cols_sb, cols), (bo_sb, bo), (bv_sb, bv),
                             (mask_sb, mask), (maskb_sb, mask_bias), (steer_sb, steer)):
                sp.dma_start(dst[:, :], src[:, :]).then_inc(consts, 16)
            for i in range(2, P1_PIECES):
                load_piece(i)

            with sp.Fori(1, GROUPS - 1) as g:
                sp.wait_ge(x_lo, 2 * g)
                load_x(g, GT)
            sp.wait_ge(x_lo, 2 * (GROUPS - 1))
            load_x(GROUPS - 1, TAIL)
            for i in range(P1_PIECES, len(PIECES)):
                load_piece(i)

            def store(g, nt):
                sp.wait_ge(out_ready, 2 * g + nt // 2)
                sp.dma_start(out[tiles_of(g, 0, nt), :, :].rearrange("t p n -> p t n"),
                             out_sb[:, 0:nt, :]).then_inc(stored, 16)

            with sp.Fori(0, GROUPS - 1) as g:
                store(g, GT)
            store(GROUPS - 1, TAIL)
            sp.wait_ge(stored, 16 * GROUPS)

        @block.gpsimd
        def _(pool):
            b1_raw = h_all[0:TREES, GT:2 * GT, :].rearrange("p t n -> p (t n)")
            b2_raw = h_all[:, 2 * GT:2 * GT + TREES, :].rearrange("p t n -> p (t n)")
            b1_parts = v_sb[0:TREES, :, :, :].rearrange("p a t n -> p (a t n)").bitcast(bf16)
            pool.dma_start(b1_raw, b1[:, :]).then_inc(bias_in, 16)
            pool.dma_start(b2_raw, b2[:, :]).then_inc(bias_in, 16)
            pool.dma_start(e_sb[:, :, :].rearrange("p t n -> p (t n)"), e_mask[:, :]).then_inc(bias_in, 16)
            pool.wait_ge(bias_in, 48)
            step = 0
            for raw, parts in ((b1_raw, [b1_parts[:, i * HID:(i + 1) * HID] for i in range(3)]),
                               (b2_raw, [b2_sb[:, i, :, :].rearrange("p t n -> p (t n)") for i in range(3)])):
                for i in range(3):
                    nc.gpsimd.tensor_copy(parts[i], raw).then_inc(bias_step, 1)
                    step += 1
                    pool.wait_ge(bias_step, step)
                    if i < 2:
                        nc.gpsimd.tensor_tensor(raw, raw, parts[i], ALU.subtract).then_inc(bias_step, 1)
                        step += 1
                        pool.wait_ge(bias_step, step)
            for i in range(3):
                for t in range(TREES):
                    pool.dma_start(e_sb[ONE_ROW + i:ONE_ROW + i + 1, t, :],
                                   b1_parts[t:t + 1, i * HID:(i + 1) * HID]).then_inc(bias_rows, 16)
            nc.gpsimd.memset(q_pad[:, :, :, :, :], 0.0).then_inc(prelude, 1)

            pool.wait_ge(consts, 16 * CONSTS)

            def add_bo(g, nt):
                pool.wait_ge(xn_ready, g + 1)
                h = h_all[0:R, tiles_of(g, 0, nt), :]
                nc.gpsimd.tensor_tensor(h, h, bo_sb[:, :].unsqueeze(1).to_broadcast([R, nt, D]), ALU.add).then_inc(bo_added, 1)

            with pool.Fori(0, GROUPS - 1) as g:
                add_bo(g, GT)
            add_bo(GROUPS - 1, TAIL)

            def split_piece(i):
                _, n, _, _, _ = PIECES[i]
                pool.wait_ge(staged[i % 2], 16 * (i // 2 + 1))
                src = stage[:, i % 2, 0:n]
                nc.gpsimd.tensor_copy(piece_dst(i, 0), src).then_inc(piece_hi, 1)
                pool.wait_ge(piece_hi, i + 1)
                nc.gpsimd.tensor_tensor(piece_dst(i, 1), src, piece_dst(i, 0).bitcast(f32), ALU.subtract).then_inc(piece_lo, 1)

            def normalise(g, nt):
                pool.wait_ge(rstd2_ready, g + 1)
                pool.wait_ge(t_done, KD * (GROUPS + g))
                cut = tiles_of(g, 0, nt)
                nc.gpsimd.tensor_tensor(xn[:, 0:nt, :], h_all[0:R, cut, :], mean2[:, cut].unsqueeze(2).to_broadcast([R, nt, D]),
                                        ALU.subtract).then_inc(centred, 1)
                pool.wait_ge(centred, g + 1)
                nc.gpsimd.tensor_tensor(xn[:, 0:nt, :], xn[:, 0:nt, :], rstd2[:, cut].unsqueeze(2).to_broadcast([R, nt, D]),
                                        ALU.mult).then_inc(xn_ready, 1)

            normalise(0, GT)
            per = 2
            at = P1_PIECES
            pool.wait_ge(tok_done, 2 * (GROUPS - 1) + TAIL // 2)
            for i in range(at, at + 2 * per):
                split_piece(i)
            pool.wait_ge(q_done, PAIRS * GROUPS)
            pool.wait_ge(k_done, PAIRS * GROUPS)
            for i in range(at + 2 * per, at + 5 * per):
                split_piece(i)
            pool.wait_ge(wo_done, PAIRS * GROUPS)
            for i in range(at + 5 * per, at + 6 * per):
                split_piece(i)
            with pool.Fori(1, GROUPS - 1) as g:
                normalise(g, GT)
            normalise(GROUPS - 1, TAIL)

        @block.scalar
        def _(act):
            def split_hi(i):
                _, n, _, _, _ = PIECES[i]
                act.wait_ge(staged[i % 2], 16 * (i // 2 + 1))
                nc.scalar.activation(piece_dst(i, 0), stage[:, i % 2, 0:n], ACT.Copy).then_inc(piece_hi, 1)

            def x_split_hi(g, half):
                if half == 0:
                    act.wait_ge(x_loaded, 16 * (g + 1))
                if not first_group(g):
                    act.wait_ge(tok_done, 2 * g)
                n = 2 * KX * R
                nc.scalar.activation(arena[:, XHI + half * n:XHI + (half + 1) * n],
                                     x_raw[:, 2 * half:2 * half + 2, :].rearrange("p t n -> p (t n)"),
                                     ACT.Copy).then_inc(x_hi, 1)

            def root(g, nt):
                act.wait_ge(var_ready, g + 1)
                nc.scalar.activation(std[:, 0:nt], mv[:, 0:nt, 1], ACT.Sqrt).then_inc(std_ready, 1)

            def transposed_hi(n, nt):
                for k in range(KD):
                    act.wait_ge(t_done, KD * n + k + 1)
                    nc.scalar.activation(xT[:, 0, k, 0:nt * R], ring[k][:, 0:nt * R], ACT.Copy).then_inc(xT_hi, 1)

            def q_evac(g, nt, j):
                act.wait_ge(q_done, PAIRS * g + j + 1)
                if j >= 2:
                    act.wait_ge(s_done, 2 * PAIRS * g + nt // 2 * (j - 1))
                for half in range(2):
                    rows = slice(HD * half, HD * (half + 1))
                    last = nc.scalar.activation(q_pad[rows, j % 2, 0:nt, half, :],
                                                ring[0][rows, 0:nt * R].rearrange("p (t r) -> p t r", r=R),
                                                ACT.Identity, bias=cols_sb[rows, j:j + 1])
                last.then_inc(q_ready, 1)

            def o_evac_hi(g, nt, j):
                if j >= 2:
                    act.wait_ge(wo_done, PAIRS * g + j - 1)
                for tp in range(nt // 2):
                    act.wait_ge(o_done, 2 * PAIRS * g + nt // 2 * j + tp + 1)
                    for half in range(2):
                        rows = slice(HD * half, HD * (half + 1))
                        src = o_ps[tp][rows, 0:2 * HW].rearrange("p (t h r) -> p t h r", t=2, h=2)
                        last = nc.scalar.activation(
                            pairT[rows, j % 2, 0, tp * HW:(tp + 1) * HW].rearrange("p (t r) -> p t r", r=R),
                            src[:, :, half, :], ACT.Copy)
                    last.then_inc(o_hi, 1)

            for i in (0, 1):
                split_hi(i)
            for half in range(2):
                x_split_hi(0, half)
            for i in (2, 3, 4, 5):
                split_hi(i)
            root(0, GT)
            transposed_hi(0, GT)
            for i in range(6, P1_PIECES):
                split_hi(i)
            act.wait_ge(consts, 16 * CONSTS)

            def attention(g, nt, nxt):
                for j in range(PAIRS + 3):
                    if j < PAIRS:
                        q_evac(g, nt, j)
                    if j in (1, 2) and 2 * (j - 1) < nxt:
                        x_split_hi(g + 1, j - 1)
                    if j == 6 and nxt:
                        root(g + 1, nxt)
                    if j == 8:
                        transposed_hi(g + 1, nxt or GT)
                    if 2 <= j < PAIRS + 2:
                        o_evac_hi(g, nt, j - 2)
                act.wait_ge(var2_ready, g + 1)
                nc.scalar.activation(std2[:, tiles_of(g, 0, nt)], var2[:, tiles_of(g, 0, nt)], ACT.Sqrt).then_inc(std2_ready, 1)

            for_groups(act, attention)

            def hidden_hi(g, nt, s):
                act.wait_ge(up_done, 3 * CH * g + s + 1)
                if s >= 3:
                    act.wait_ge(down_done, 3 * CH * g + s - 2)
                nc.scalar.activation(pairT[:, s % 3, 0, 0:nt * R], hid_ps[s % 3][:, 0:nt * R], ACT.Relu).then_inc(hid_hi, 1)

            def probs_out(g, nt):
                act.wait_ge(pt_done, g + 1)
                nc.scalar.activation(probsT[:, 0:nt * R], ring[1][0:R, 0:nt * R], ACT.Copy).then_inc(pt_ready, 1)

            def ffn(g, nt, nxt, first=False):
                for s in range(TREES * CH + 2):
                    if s < TREES * CH:
                        hidden_hi(g, nt, s)
                    for tree in range(2):
                        if s == CH * (tree + 1) + 1:
                            act.wait_ge(down_done, 3 * CH * g + CH * (tree + 1))
                            for m in range(KD):
                                last = nc.scalar.activation(qT[:, tree, m, 0:nt * R], down[m][:, 0:nt * R], ACT.Copy)
                            last.then_inc(down_q, 1)
                    if s == 3 and not first:
                        probs_out(g - 1, GT)
                    if s == TREES * CH and nxt:
                        transposed_hi(GROUPS + g + 1, nxt)
                exps(g, nt)

            def exps(g, nt):
                act.wait_ge(max_ready, g + 1)
                for t in range(nt):
                    last = nc.scalar.activation(probs[:, t * R:(t + 1) * R], soft_in[:, t * R:(t + 1) * R], ACT.Exp,
                                                bias=neg_max[:, t:t + 1], accum_out=row_sum[:, t:t + 1])
                last.then_inc(exp_ready, 1)

            ffn(0, GT, GT, first=True)
            with act.Fori(1, GROUPS - 2) as g:
                ffn(g, GT, GT)
            ffn(GROUPS - 2, GT, TAIL)
            ffn(GROUPS - 1, TAIL, 0)
            probs_out(GROUPS - 1, TAIL)

        @block.vector
        def _(dve):
            def split_lo(i):
                _, n, _, _, _ = PIECES[i]
                dve.wait_ge(piece_hi, i + 1)
                nc.vector.tensor_tensor(piece_dst(i, 1), stage[:, i % 2, 0:n], piece_dst(i, 0).bitcast(f32),
                                        ALU.subtract).then_inc(piece_lo, 1)

            def x_split_lo(g, half):
                dve.wait_ge(x_hi, 2 * g + half + 1)
                n = 2 * KX * R
                nc.vector.tensor_tensor(arena[:, XLO + half * n:XLO + (half + 1) * n],
                                        x_raw[:, 2 * half:2 * half + 2, :].rearrange("p t n -> p (t n)"),
                                        arena[:, XHI + half * n:XHI + (half + 1) * n].bitcast(f32),
                                        ALU.subtract).then_inc(x_lo, 1)

            def embed(g, nt):
                for tp in range(nt // 2):
                    dve.wait_ge(tok_done, 2 * g + tp + 1)
                    nc.vector.tensor_tensor(h_all[0:R, tiles_of(g, 2 * tp, 2), :],
                                            ring[tp][0:R, :].rearrange("p (t n) -> p t n", t=2),
                                            pos_sb[:, :].unsqueeze(1).to_broadcast([R, 2, D]), ALU.add).then_inc(h_ready, 1)

            def moments(g, nt):
                base = 0 if first_group(g) else 5 * g - 2
                dve.wait_ge(h_ready, 2 * g + nt // 2)
                nc.vector.memset(bearer[:, 0:1], 0.0)
                for t in range(nt):
                    last = nc.vector.bn_stats(stats[:, t, :], h_all[0:R, tiles_of(g, t, 1), :].rearrange("p t n -> p (t n)"))
                last.then_inc(stat_step, 1)
                dve.wait_ge(stat_step, base + 1)
                nc.vector.memset(bearer[:, 1:2], 0.0)
                for t in range(nt):
                    last = nc.vector.bn_aggr(mv[:, t, :], stats[:, t, :])
                last.then_inc(stat_step, 1)
                dve.wait_ge(stat_step, base + 2)
                nc.vector.tensor_scalar(mv[:, 0:nt, 1], mv[:, 0:nt, 1], EPS, None, ALU.add).then_inc(var_ready, 1)

            def normalise(g, nt):
                dve.wait_ge(std_ready, g + 1)
                nc.vector.reciprocal(rstd[:, 0:nt], std[:, 0:nt]).then_inc(stat_step, 1)
                dve.wait_ge(stat_step, 3 if first_group(g) else 5 * g + 1)
                if not first_group(g):
                    dve.wait_ge(t_done, KD * g)
                for t in range(nt):
                    last = nc.vector.tensor_scalar(xn[:, t, :], h_all[0:R, tiles_of(g, t, 1), :].rearrange("p t n -> p (t n)"),
                                                   mv[:, t, 0:1], rstd[:, t:t + 1], ALU.subtract, ALU.mult)
                last.then_inc(xn_ready, 1)

            def transposed_lo(n, nt):
                for k in range(KD):
                    dve.wait_ge(xT_hi, KD * n + k + 1)
                    nc.vector.tensor_tensor(xT[:, 1, k, 0:nt * R], ring[k][:, 0:nt * R],
                                            xT[:, 0, k, 0:nt * R].bitcast(f32), ALU.subtract).then_inc(xT_lo, 1)

            def v_evac(g, nt, quarter):
                if quarter >= 2:
                    dve.wait_ge(o_done, 2 * PAIRS * g + nt // 2 * (2 * quarter - 2))
                for tp in range(nt // 2):
                    dve.wait_ge(v_done, PAIRS * g + nt // 2 * quarter + tp + 1)
                    nc.vector.tensor_tensor(v_sb[0:R, quarter % 2, 2 * tp:2 * tp + 2, :],
                                            ring[tp][0:R, :].rearrange("p (t n) -> p t n", t=2),
                                            bv_sb[:, quarter * D:(quarter + 1) * D].unsqueeze(1).to_broadcast([R, 2, D]),
                                            ALU.add).then_inc(v_ready, 1)

            def k_evac(g, nt, j):
                dve.wait_ge(k_done, PAIRS * g + j + 1)
                if j >= 2:
                    dve.wait_ge(s_done, 2 * PAIRS * g + nt // 2 * (j - 1))
                nc.vector.tensor_scalar(k_sb[:, j % 2, 0:nt * R], ring[1][:, 0:nt * R], cols_sb[:, PAIRS + j:PAIRS + j + 1],
                                        None, ALU.add).then_inc(k_ready, 1)

            def s_evac(g, nt, j):
                if j >= 2:
                    dve.wait_ge(o_done, 2 * PAIRS * g + nt // 2 * (j - 1))
                for tp in range(nt // 2):
                    dve.wait_ge(s_done, 2 * PAIRS * g + nt // 2 * j + tp + 1)
                    nc.vector.tensor_tensor(s_sb[:, j % 2, 2 * tp:2 * tp + 2, :].rearrange("p t (h r) -> p (t h) r", h=2),
                                            s_ps[tp][0:R, 0:2 * HW].rearrange("p (b r) -> p b r", r=R),
                                            mask_sb[:, :].unsqueeze(1).to_broadcast([R, 4, R]), ALU.mult).then_inc(s_ready, 1)

            def o_evac_lo(g, nt, j):
                for tp in range(nt // 2):
                    dve.wait_ge(o_hi, 2 * PAIRS * g + nt // 2 * j + tp + 1)
                    for half in range(2):
                        rows = slice(HD * half, HD * (half + 1))
                        src = o_ps[tp][rows, 0:2 * HW].rearrange("p (t h r) -> p t h r", t=2, h=2)
                        cut = slice(tp * HW, (tp + 1) * HW)
                        last = nc.vector.tensor_tensor(
                            pairT[rows, j % 2, 1, cut].rearrange("p (t r) -> p t r", r=R), src[:, :, half, :],
                            pairT[rows, j % 2, 0, cut].bitcast(f32).rearrange("p (t r) -> p t r", r=R), ALU.subtract)
                    last.then_inc(o_lo, 1)

            def residual(g, nt):
                dve.wait_ge(wo_done, PAIRS * (g + 1))
                dve.wait_ge(bo_added, g + 1)
                for tp in range(nt // 2):
                    h = h_all[0:R, tiles_of(g, 2 * tp, 2), :]
                    nc.vector.tensor_tensor(h, wo_acc[tp][0:R, :].rearrange("p (t n) -> p t n", t=2), h, ALU.add).then_inc(h2_ready, 1)
                dve.wait_ge(h2_ready, 2 * g + nt // 2)
                nc.vector.memset(bearer[:, 0:1], 0.0)
                for t in range(nt):
                    last = nc.vector.bn_stats(stats[:, t, :], h_all[0:R, tiles_of(g, t, 1), :].rearrange("p t n -> p (t n)"))
                last.then_inc(stat_step, 1)
                dve.wait_ge(stat_step, stat_base(g, nt) + 1)
                nc.vector.memset(bearer[:, 1:2], 0.0)
                for t in range(nt):
                    last = nc.vector.bn_aggr(mv[:, t, :], stats[:, t, :])
                last.then_inc(stat_step, 1)
                dve.wait_ge(stat_step, stat_base(g, nt) + 2)
                nc.vector.tensor_copy(mean2[:, tiles_of(g, 0, nt)], mv[:, 0:nt, 0])
                nc.vector.tensor_scalar(var2[:, tiles_of(g, 0, nt)], mv[:, 0:nt, 1], EPS, None, ALU.add).then_inc(var2_ready, 1)
                dve.wait_ge(std2_ready, g + 1)
                nc.vector.reciprocal(rstd2[:, tiles_of(g, 0, nt)], std2[:, tiles_of(g, 0, nt)]).then_inc(rstd2_ready, 1)

            def stat_base(g, nt):
                return 5 * g + (6 if nt == GT else 3)

            for i in (0, 1):
                split_lo(i)
            for half in range(2):
                x_split_lo(0, half)
            for i in (2, 3):
                split_lo(i)
            dve.wait_ge(consts, 16 * CONSTS)
            nc.vector.tensor_tensor(pos_sb[:, :], pos_sb[:, :], xn[:, 0, :], ALU.add).then_inc(pos_ready, 1)
            dve.wait_ge(pos_ready, 1)
            embed(0, GT)
            moments(0, GT)
            for i in (4, 5):
                split_lo(i)
            normalise(0, GT)
            transposed_lo(0, GT)
            for i in range(6, P1_PIECES):
                split_lo(i)
            dve.wait_ge(bias_rows, 16 * 3 * TREES)

            def attention(g, nt, nxt):
                for j in range(PAIRS + 3):
                    if j < PAIRS:
                        if j % 2 == 0:
                            v_evac(g, nt, j // 2)
                        if j == 5 and nxt:
                            embed(g + 1, nxt)
                        k_evac(g, nt, j)
                    if j in (1, 2) and 2 * (j - 1) < nxt:
                        x_split_lo(g + 1, j - 1)
                    if j == 8:
                        transposed_lo(g + 1, nxt or GT)
                    if 1 <= j < PAIRS + 1:
                        s_evac(g, nt, j - 1)
                    if 2 <= j < PAIRS + 2:
                        o_evac_lo(g, nt, j - 2)
                    if j == 5 and nxt:
                        moments(g + 1, nxt)
                    if j == 6 and nxt:
                        normalise(g + 1, nxt)
                residual(g, nt)

            for_groups(dve, attention)

            def route_bits(g, nt):
                dve.wait_ge(score_done, g + 1)
                nc.vector.tensor_scalar(bitsT[:, 0:nt * R], ring[0][:, 0:nt * R], cols_sb[:, 2 * PAIRS:2 * PAIRS + 1], 0.0,
                                        ALU.add, ALU.is_ge).then_inc(bits_ready, 1)

            def route(g, nt):
                dve.wait_ge(count_done, g + 1)
                nc.vector.tensor_scalar(routeT[:, 0:nt * R], ring[1][:, 0:nt * R], cols_sb[:, 2 * PAIRS + 1:2 * PAIRS + 2],
                                        None, ALU.is_ge).then_inc(route_ready, 1)

            def hidden_lo(g, nt, s):
                dve.wait_ge(hid_hi, 3 * CH * g + s + 1)
                nc.vector.scalar_tensor_tensor(pairT[:, s % 3, 1, 0:nt * R], hid_ps[s % 3][:, 0:nt * R], 0.0,
                                               pairT[:, s % 3, 0, 0:nt * R].bitcast(f32), ALU.max, ALU.subtract).then_inc(hid_lo, 1)

            def softmax_in(g, nt):
                dve.wait_ge(att_done, g + 1)
                nc.vector.scalar_tensor_tensor(soft_in[:, 0:nt * R].rearrange("p (t r) -> p t r", r=R),
                                               ring[0][0:R, 0:nt * R].rearrange("p (t r) -> p t r", r=R), float(D) ** -0.5,
                                               maskb_sb[:, :].unsqueeze(1).to_broadcast([R, nt, R]),
                                               ALU.mult, ALU.add).then_inc(soft_step, 1)
                dve.wait_ge(soft_step, 3 * g + 1)
                nc.vector.tensor_reduce(row_inv[:, 0:nt], soft_in[:, 0:nt * R].rearrange("p (t r) -> p t r", r=R),
                                        AX.X, ALU.max).then_inc(soft_step, 1)
                dve.wait_ge(soft_step, 3 * g + 2)
                nc.vector.tensor_scalar(neg_max[:, 0:nt], row_inv[:, 0:nt], -1.0, None, ALU.mult).then_inc(max_ready, 1)

            def finish(g, nt):
                dve.wait_ge(exp_ready, g + 1)
                nc.vector.reciprocal(row_inv[:, 0:nt], row_sum[:, 0:nt]).then_inc(soft_step, 1)
                dve.wait_ge(soft_step, 3 * g + 3)
                if not first_group(g):
                    dve.wait_ge(stored, 16 * g)
                for tp in range(nt // 2):
                    dve.wait_ge(av_done, 2 * g + tp + 1)
                    for t in (2 * tp, 2 * tp + 1):
                        last = nc.vector.scalar_tensor_tensor(out_sb[:, t, :], ring[tp][0:R, t % 2 * D:(t % 2 + 1) * D],
                                                              row_inv[:, t:t + 1],
                                                              h_all[0:R, tiles_of(g, t, 1), :].rearrange("p t n -> p (t n)"),
                                                              ALU.mult, ALU.add)
                    last.then_inc(out_ready, 1)

            route_bits(0, GT)
            route(0, GT)

            def ffn(g, nt, nxt, first=False):
                for s in range(TREES * CH + 2):
                    if s < TREES * CH:
                        hidden_lo(g, nt, s)
                    if s == 5 and not first:
                        finish(g - 1, GT)
                    if s == TREES * CH and nxt:
                        transposed_lo(GROUPS + g + 1, nxt)
                dve.wait_ge(down_done, 3 * CH * (g + 1))
                for tp in range(nt // 2):
                    last = nc.vector.tensor_copy(v2[:, 2 * tp:2 * tp + 2, :], down[tp][0:R, :].rearrange("p (t n) -> p t n", t=2))
                last.then_inc(down_v, 1)
                if nxt:
                    route_bits(g + 1, nxt)
                softmax_in(g, nt)
                if nxt:
                    route(g + 1, nxt)

            ffn(0, GT, GT, first=True)
            with dve.Fori(1, GROUPS - 2) as g:
                ffn(g, GT, GT)
            ffn(GROUPS - 2, GT, TAIL)
            ffn(GROUPS - 1, TAIL, 0)
            finish(GROUPS - 1, TAIL)

        @block.tensor
        def _(pe):
            def embed(g, nt):
                for t in range(nt):
                    if t % 2 == 0:
                        pe.wait_ge(x_lo, 2 * g + t // 2 + 1)
                    for k in range(KX):
                        for n, (a, b) in enumerate(PRODUCTS):
                            at = (XLO if a else XHI) + t * KX * R + k * R
                            last = nc.tensor.matmul(ring[t // 2][0:R, t % 2 * D:(t % 2 + 1) * D], arena[:, at:at + R],
                                                    tok_w(k, b), start=(k == n == 0), stop=(k == KX - 1 and n == 2),
                                                    skip_group_check=True)
                    if t % 2:
                        last.then_inc(tok_done, 1)

            def turn(n, nt):
                pe.wait_ge(xn_ready, n + 1)
                for k in range(KD):
                    for t in range(nt):
                        last = nc.tensor.transpose(ring[k][:, t * R:(t + 1) * R], xn[:, t, k * 128:(k + 1) * 128],
                                                   id_sb[0:R, 0:R])
                    last.then_inc(t_done, 1)

            def values(g, nt, quarter):
                if quarter == 0:
                    pe.wait_ge(xT_lo, KD * (g + 1))
                for t in range(nt):
                    if t % 2 == 0 and quarter:
                        pe.wait_ge(k_ready if t else q_ready, PAIRS * g + 2 * quarter)
                    n = 0
                    for k in range(KD):
                        for a, b in PRODUCTS:
                            last = nc.tensor.matmul(ring[t // 2][0:R, t % 2 * D:(t % 2 + 1) * D],
                                                    xT[:, a, k, t * R:(t + 1) * R], in_w(WV, k, quarter * D, D, b),
                                                    start=(n == 0), stop=(n == 5), skip_group_check=True)
                            n += 1
                    if t % 2:
                        last.then_inc(v_done, 1)

            def project(g, nt, j, bank, base, done):
                n = 0
                for k in range(KD):
                    for a, b in PRODUCTS:
                        last = nc.tensor.matmul(ring[bank][:, 0:nt * R], in_w(base, k, 128 * j, 128, a),
                                                xT[:, b, k, 0:nt * R], start=(n == 0), stop=(n == 5))
                        n += 1
                last.then_inc(done, 1)

            def scores(g, nt, j):
                pe.wait_ge(q_ready, PAIRS * g + j + 1)
                pe.wait_ge(k_ready, PAIRS * g + j + 1)
                for t in range(nt):
                    if t % 2 == 0:
                        if j:
                            pe.wait_ge(s_ready, 2 * PAIRS * g + nt // 2 * (j - 1) + t // 2 + 1)
                    last = nc.tensor.matmul(s_ps[t // 2][0:R, t % 2 * 2 * R:(t % 2 + 1) * 2 * R],
                                            k_sb[:, j % 2, t * R:(t + 1) * R],
                                            q_pad[:, j % 2, t, :, :].rearrange("p h r -> p (h r)"),
                                            start=True, stop=True, skip_group_check=True)
                    if t % 2:
                        last.then_inc(s_done, 1)

            def mix(g, nt, j):
                pe.wait_ge(v_ready, PAIRS * g + nt // 2 * (j // 2 + 1))
                for t in range(nt):
                    if t % 2 == 0:
                        pe.wait_ge(s_ready, 2 * PAIRS * g + nt // 2 * j + t // 2 + 1)
                        if j:
                            pe.wait_ge(o_lo, 2 * PAIRS * g + nt // 2 * (j - 1) + t // 2 + 1)
                    last = nc.tensor.matmul(o_ps[t // 2][:, t % 2 * 2 * R:(t % 2 + 1) * 2 * R],
                                            v_sb[0:R, j // 2 % 2, t, j % 2 * 128:(j % 2 + 1) * 128],
                                            s_sb[:, j % 2, t, :], start=True, stop=True, skip_group_check=True)
                    if t % 2:
                        last.then_inc(o_done, 1)

            def project_out(g, nt, j):
                pe.wait_ge(o_lo, 2 * PAIRS * g + nt // 2 * (j + 1))
                if j == 0 and not first_group(g):
                    pe.wait_ge(h2_ready, 2 * g)
                for t in range(nt):
                    for n, (a, b) in enumerate(PRODUCTS):
                        last = nc.tensor.matmul(wo_acc[t // 2][0:R, t % 2 * D:(t % 2 + 1) * D],
                                                pairT[:, j % 2, a, t * R:(t + 1) * R], out_w(WO, j, 0, D, b),
                                                start=(j == 0 and n == 0 and t % 2 == 0),
                                                stop=(j == PAIRS - 1 and n == 2), skip_group_check=True)
                last.then_inc(wo_done, 1)

            def node_scores(g, nt):
                pe.wait_ge(xT_lo, KD * (GROUPS + g + 1))
                n = 0
                for k in range(KD):
                    for a, b in PRODUCTS:
                        last = nc.tensor.matmul(ring[0][:, 0:nt * R], node_w[:, a, k, :], xT[:, b, k, 0:nt * R],
                                                start=(n == 0), stop=(n == 5))
                        n += 1
                last.then_inc(score_done, 1)

            def path_counts(g, nt):
                pe.wait_ge(bits_ready, g + 1)
                nc.tensor.matmul(ring[1][:, 0:nt * R], steer_sb[:, :], bitsT[:, 0:nt * R],
                                 start=True, stop=True).then_inc(count_done, 1)

            pe.wait_ge(piece_lo, pieces_until(WT))
            embed(0, GT)
            pe.wait_ge(consts, 16 * CONSTS)
            turn(0, GT)
            pe.wait_ge(piece_lo, P1_PIECES)
            pe.wait_ge(prelude, 1)

            def attention(g, nt, nxt):
                for j in range(PAIRS + 3):
                    if j < PAIRS:
                        if j % 2 == 0:
                            values(g, nt, j // 2)
                        if j == 5 and nxt:
                            pe.wait_ge(q_ready, PAIRS * g + j)
                            pe.wait_ge(k_ready, PAIRS * g + j)
                            embed(g + 1, nxt)
                        if j % 2 == 0:
                            pe.wait_ge(v_ready, PAIRS * g + nt // 2 * (j // 2) + 1)
                        elif j == 5 and nxt:
                            pe.wait_ge(h_ready, 2 * (g + 1) + 1)
                        else:
                            pe.wait_ge(q_ready, PAIRS * g + j)
                        project(g, nt, j, 0, WQ, q_done)
                        if j % 2 == 0 and nt == GT:
                            pe.wait_ge(v_ready, PAIRS * g + nt // 2 * (j // 2) + 2)
                        elif j == 5 and nxt == GT:
                            pe.wait_ge(h_ready, 2 * (g + 1) + 2)
                        elif j:
                            pe.wait_ge(k_ready, PAIRS * g + j)
                        project(g, nt, j, 1, WK, k_done)
                    if j == 8:
                        pe.wait_ge(q_ready, PAIRS * (g + 1))
                        pe.wait_ge(k_ready, PAIRS * (g + 1))
                        turn(g + 1, nxt or GT)
                    if 1 <= j < PAIRS + 1:
                        scores(g, nt, j - 1)
                    if 2 <= j < PAIRS + 2:
                        mix(g, nt, j - 2)
                    if j >= 3:
                        project_out(g, nt, j - 3)

            for_groups(pe, attention)

            pe.wait_ge(h2_ready, 2 * (GROUPS - 1) + TAIL // 2)

            def up(g, nt, s):
                tree, c = s // CH, s % CH
                if s >= 3:
                    pe.wait_ge(hid_lo, 3 * CH * g + s - 2)
                elif not first_group(g):
                    pe.wait_ge(hid_lo, 3 * CH * g)
                n = 0
                for k in range(KD):
                    for a, b in PRODUCTS:
                        nc.tensor.matmul(hid_ps[s % 3][:, 0:nt * R], in_w(W1[tree], k, 128 * c, 128, a),
                                         xT[:, b, k, 0:nt * R], start=(n == 0), stop=False)
                        n += 1
                if s == 0:
                    pe.wait_ge(route_ready, g + 1)
                nc.tensor.matmul(hid_ps[s % 3][:, 0:nt * R], e_sb[:, tree, 128 * c:128 * (c + 1)], routeT[:, 0:nt * R],
                                 start=False, stop=True).then_inc(up_done, 1)

            def down_step(g, nt, s):
                tree, c = s // CH, s % CH
                pe.wait_ge(hid_lo, 3 * CH * g + s + 1)
                if c == 0 and tree:
                    pe.wait_ge(down_q, 2 * g + tree)
                elif c == 0 and not first_group(g):
                    pe.wait_ge(down_v, g)
                if tree < 2:
                    for m in range(KD):
                        for n, (a, b) in enumerate(PRODUCTS):
                            last = nc.tensor.matmul(down[m][:, 0:nt * R], out_w(W2[tree], c, 128 * m, 128, a),
                                                    pairT[:, s % 3, b, 0:nt * R], start=(c == n == 0), stop=False,
                                                    skip_group_check=True)
                        for p in range(3 * (c == CH - 1)):
                            last = nc.tensor.matmul(down[m][:, 0:nt * R], b2_sb[:, p, tree, 128 * m:128 * (m + 1)],
                                                    routeT[:, 0:nt * R], start=False, stop=(p == 2), skip_group_check=True)
                else:
                    for t in range(nt):
                        acc = down[t // 2][0:R, t % 2 * D:(t % 2 + 1) * D]
                        for n, (a, b) in enumerate(PRODUCTS):
                            last = nc.tensor.matmul(acc, pairT[:, s % 3, a, t * R:(t + 1) * R], out_w(W2[tree], c, 0, D, b),
                                                    start=(c == n == 0 and t % 2 == 0), stop=False, skip_group_check=True)
                        for p in range(3 * (c == CH - 1)):
                            last = nc.tensor.matmul(acc, routeT[:, t * R:(t + 1) * R], b2_sb[:, p, tree, :],
                                                    start=False, stop=(p == 2), skip_group_check=True)
                last.then_inc(down_done, 1)

            def attend(g, nt):
                pe.wait_ge(down_q, 2 * (g + 1))
                for t in range(nt):
                    for k in range(KD):
                        last = nc.tensor.matmul(ring[0][0:R, t * R:(t + 1) * R], qT[:, 0, k, t * R:(t + 1) * R],
                                                qT[:, 1, k, t * R:(t + 1) * R], start=(k == 0), stop=(k == KD - 1),
                                                skip_group_check=True)
                last.then_inc(att_done, 1)

            def turn_probs(g, nt):
                pe.wait_ge(exp_ready, g + 1)
                for t in range(nt):
                    last = nc.tensor.transpose(ring[1][0:R, t * R:(t + 1) * R], probs[:, t * R:(t + 1) * R], id_sb[0:R, 0:R])
                last.then_inc(pt_done, 1)

            def weigh(g, nt):
                pe.wait_ge(pt_ready, g + 1)
                pe.wait_ge(down_v, g + 1)
                for t in range(nt):
                    last = nc.tensor.matmul(ring[t // 2][0:R, t % 2 * D:(t % 2 + 1) * D], probsT[:, t * R:(t + 1) * R],
                                            v2[:, t, :], start=True, stop=True, skip_group_check=True)
                    if t % 2:
                        last.then_inc(av_done, 1)

            pe.wait_ge(piece_lo, pieces_until(NODE_W))
            node_scores(0, GT)
            path_counts(0, GT)
            pe.wait_ge(bias_rows, 16 * 3 * TREES)

            def ffn(g, nt, nxt, first=False):
                for s in range(TREES * CH + 2):
                    if first and s % CH == 0 and s < TREES * CH:
                        pe.wait_ge(piece_lo, P1_PIECES + (s // CH) * 4 + 2)
                    if first and s % CH == 2 and s < TREES * CH:
                        pe.wait_ge(piece_lo, P1_PIECES + (s // CH) * 4 + 4)
                    if s < TREES * CH:
                        up(g, nt, s)
                    if s == 3 and not first:
                        pe.wait_ge(route_ready, g + 1)
                        turn_probs(g - 1, GT)
                    if s == 5 and not first:
                        weigh(g - 1, GT)
                    if s == TREES * CH and nxt:
                        if not first:
                            pe.wait_ge(out_ready, 2 * g)
                        turn(GROUPS + g + 1, nxt)
                    if s >= 2:
                        down_step(g, nt, s - 2)
                if nxt:
                    node_scores(g + 1, nxt)
                    pe.wait_ge(bits_ready, g + 2)
                elif not first:
                    pe.wait_ge(out_ready, 2 * g)
                attend(g, nt)
                if nxt:
                    path_counts(g + 1, nxt)

            ffn(0, GT, GT, first=True)
            with pe.Fori(1, GROUPS - 2) as g:
                ffn(g, GT, GT)
            ffn(GROUPS - 2, GT, TAIL)
            ffn(GROUPS - 1, TAIL, 0)
            turn_probs(GROUPS - 1, TAIL)
            weigh(GROUPS - 1, TAIL)


def launch_arrays(i):
    f = np.float32
    x = np.zeros((TILES * PER_TILE,) + i["x"].shape[1:], f)
    x[:IMAGES] = i["x"]
    n = SIDE // PATCH
    x = x.reshape(TILES, PER_TILE, CHANNELS, n, PATCH, n, PATCH).transpose(0, 2, 4, 6, 1, 3, 5)
    x = x.reshape(TILES, KX, 128, PER_TILE * PATCHES).transpose(0, 2, 1, 3)
    xt = np.zeros((TILES, 128, KX, ROWS), f)
    xt[..., :PER_TILE * PATCHES] = x

    def chunks(w):
        return w.reshape(-1, 128, w.shape[1]).transpose(1, 0, 2).reshape(128, -1)

    def padded(w, rows):
        return np.concatenate([w, np.zeros((rows - w.shape[0],) + w.shape[1:], w.dtype)])

    trees = "qkv"
    node_w = np.concatenate([padded(i[f"L0_ffn_{t}_node_w"], LEAVES) for t in trees])
    mats = [chunks(i["L0_tok_W"].T)] + [chunks(i[f"L0_attn_W{c}"]) for c in "vqk"]
    mats += [chunks(padded(node_w, 128).T), chunks(i["L0_attn_Wo"])]
    for t in trees:
        mats += [chunks(i[f"L0_ffn_{t}_w1"].transpose(1, 0, 2).reshape(D, HID)), chunks(i[f"L0_ffn_{t}_w2"].reshape(HID, D))]
    weights = np.concatenate(mats, 1)

    patch_rows, real = PER_TILE * PATCHES, PER_TILE * (PATCHES + 1)
    p = i["L0_tok_pos_embedding"][0]
    pos = np.zeros((2, ROWS, D), f)
    pos[0, :patch_rows] = np.tile(p[1:], (PER_TILE, 1))
    pos[0, patch_rows:real] = p[0]
    pos[1, :patch_rows] = i["L0_tok_b"]
    pos[1, patch_rows:real] = i["L0_tok_cls_token"][0, 0]
    image = np.concatenate([np.arange(patch_rows) // PATCHES, np.arange(ROWS - patch_rows)])
    same = image[:, None] == image[None, :]

    node_b = np.full((128,), -1.0, f)
    for t, c in enumerate(trees):
        node_b[LEAVES * t:LEAVES * t + NODES] = i[f"L0_ffn_{c}_node_b"]
    steer = np.zeros((128, 128), f)
    thr = np.ones((128,), f)
    thr[ONE_ROW:ONE_ROW + 3] = 0.0
    e_mask = np.zeros((128, TREES, LEAVES, LEAF_W), f)
    for t in range(TREES):
        for leaf in range(LEAVES):
            off, sel = OFF_ROW + LEAVES * t + leaf, SEL_ROW + LEAVES * t + leaf
            node, rights = leaf + NODES, 0
            while node:
                parent = (node - 1) // 2
                right = node == 2 * parent + 2
                rights += right
                steer[LEAVES * t + parent, sel] = 1.0 if right else -1.0
                node = parent
            steer[:, off] = -steer[:, sel]
            thr[sel], thr[off] = rights, 1 - rights
            e_mask[off, t, leaf] = -BIG
    cols = np.stack([*i["L0_attn_bq"].reshape(PAIRS, 128), *i["L0_attn_bk"].reshape(PAIRS, 128), node_b, thr], 1)
    b2 = np.zeros((128, TREES, D), f)
    for t, c in enumerate(trees):
        b2[SEL_ROW + LEAVES * t:SEL_ROW + LEAVES * (t + 1), t] = i[f"L0_ffn_{c}_b2"]
    bf = mybir.dt.np(mybir.dt.bfloat16)
    return dict(
        x=xt.reshape(TILES, 128, -1), weights=weights, pos=pos[0], tok=pos[1], ident=np.eye(128, dtype=f),
        mask=np.where(same, f(HD ** -0.5), f(0)), mask_bias=np.where(same, f(0), f(-1e30)),
        bv=np.tile(i["L0_attn_bv"], (ROWS, 1)), bo=np.tile(i["L0_attn_bo"], (ROWS, 1)), cols=cols.astype(f),
        e_mask=e_mask.reshape(128, -1).astype(bf), b1=np.stack([i[f"L0_ffn_{c}_b1"].reshape(-1) for c in trees]),
        b2=b2.reshape(128, -1), steer=steer.astype(bf))


def kernel(**inputs):
    import concourse.bacc as bacc
    from concourse.bass_utils import run_bass_kernel_spmd

    arrays = {k: np.ascontiguousarray(v) for k, v in launch_arrays({k: np.asarray(v) for k, v in inputs.items()}).items()}
    nc = bacc.Bacc("TRN2", target_bir_lowering=False, num_devices=1)
    args = {k: nc.dram_tensor(k, a.shape, mybir.dt.from_np(a.dtype), kind="ExternalInput").ap() for k, a in arrays.items()}
    out = nc.dram_tensor("out", (TILES, ROWS, D), mybir.dt.float32, kind="ExternalOutput").ap()
    build_program(nc, *args.values(), out)
    got = run_bass_kernel_spmd(nc, [arrays], core_ids=[0]).results[0]["out"]
    patch_rows, real = PER_TILE * PATCHES, PER_TILE * (PATCHES + 1)
    patches = got[:, :patch_rows].reshape(TILES * PER_TILE, PATCHES, D)
    return np.concatenate([got[:, patch_rows:real].reshape(TILES * PER_TILE, 1, D), patches], 1)[:IMAGES]
```

```python
import concourse.bass as bass
from concourse import mybir
from contextlib import ExitStack
import numpy as np

IMAGES, CHANNELS, SIDE, PATCH, D = 64, 3, 96, 16, 256
PATCHES = (SIDE // PATCH) ** 2
PER_TILE = 3
ROWS = PER_TILE * (PATCHES + 1) + 1
TILES = -(-IMAGES // PER_TILE)
GT = 4
GROUPS = -(-TILES // GT)
TAIL = TILES - GT * (GROUPS - 1)
W = GT * ROWS
KX = CHANNELS * PATCH * PATCH // 128
KD = D // 128
HEADS, HD = 16, 64
PAIRS = HEADS // 2
INNER = HEADS * HD
TREES, LEAVES, NODES, LEAF_W, DEPTH = 3, 16, 15, 64, 4
HID = LEAVES * LEAF_W
CH = HID // 128
BIG = 2.0 ** 126
EPS = 1e-5

OFF_ROW = 0
ONE_ROW = 48
SEL_ROWS = (0, 64)

XHI, XLO = 0, GT * KX * ROWS
WT = 2 * GT * KX * ROWS
WQ = WT + 2 * KX * D
WSIZE = 2 * KD * INNER
WK, WV, WO = WQ + WSIZE, WQ + 2 * WSIZE, WQ + 3 * WSIZE
ARENA = WO + WSIZE
W1 = [0, WQ, WV]
W2 = [WSIZE, WK, WO]

STAGE = 1024
NODE_W = -1
PIECES, _at = [], 0
_HALVES = [(w, WSIZE // 2, half * STAGE, STAGE) for half in range(2) for w in (WV, WQ, WK, WO)]
_TREES = [(w, WSIZE // 2, half * STAGE, STAGE) for t in range(TREES) for w in (W1[t], W2[t]) for half in range(2)]
for _dst, _size, _off, _n in [(WT, KX * D, 0, STAGE), (WT, KX * D, STAGE, KX * D - STAGE), *_HALVES,
                              (NODE_W, KD * 128, 0, KD * 128), *_TREES]:
    PIECES.append((_at, _n, _dst, _size, _off))
    _at += _n
WT_PIECES = 2
HALF_PIECES = 4
P1_PIECES = WT_PIECES + 2 * HALF_PIECES + 1
SLOTS = 4


CONSTS = 4
CONSTS2 = 5


def first_group(g):
    return isinstance(g, int) and g == 0


def build_program(nc, x, weights, pos, tok, ident, mask, mask_bias, bv, bo, cols, e_mask, b1, b2, steer, out):
    f32, f32r, bf16 = mybir.dt.float32, mybir.dt.float32r, mybir.dt.bfloat16
    ALU, ACT, AX = mybir.AluOpType, mybir.ActivationFunctionType, mybir.AxisListType
    R = ROWS
    HW = GT * R // 2

    with ExitStack() as ctx:
        def sb(name, shape, dt=f32):
            return ctx.enter_context(nc.sbuf_tensor("sb_" + name, shape, dt))

        def sem(name):
            return ctx.enter_context(nc.semaphore(name))

        arena = sb("arena", [128, ARENA], f32r)
        node_w = sb("node_w", [128, 2, KD, 128], f32r)
        xT = sb("xT", [128, 2, KD, W], f32r)
        pairT = sb("pairT", [128, 3, 2, W], f32r)
        e_sb = sb("e_sb", [128, TREES, HID], bf16)
        b2_sb = sb("b2_sb", [128, TREES, D], f32r)
        routeT = sb("routeT", [128, W], bf16)
        selT = sb("selT", [128, W], f32r)
        bitsT = sb("bitsT", [128, W], bf16)
        steer_sb = sb("steer_sb", [128, 256], bf16)
        x_raw = sb("x_raw", [128, GT, KX * R])
        stage = sb("stage", [128, 2, STAGE])
        h_all = sb("h_all", [128, TILES, D])
        xn = sb("xn", [R, GT, D])
        q_pad = sb("q_pad", [128, 2, GT, 2, R])
        k_sb = sb("k_sb", [128, 2, W])
        v_sb = sb("v_sb", [128, 2, GT, D])
        s_sb = sb("s_sb", [R, 2, GT, 2 * R])
        bv_sb = sb("bv_sb", [R, INNER])
        bo_sb = sb("bo_sb", [R, D])
        pos_sb = sb("pos_sb", [R, D])
        mask_sb = sb("mask_sb", [R, R])
        maskb_sb = sb("maskb_sb", [R, R])
        id_sb = sb("id_sb", [128, 128])
        cols_sb = sb("cols_sb", [128, 2 * PAIRS + 3])
        stats = sb("stats", [R, GT, 6])
        mv = sb("mv", [R, GT, 2])
        bearer = sb("bearer", [R, 2])
        std = sb("std", [R, GT])
        rstd = sb("rstd", [R, GT])
        mean2 = sb("mean2", [R, TILES])
        var2 = sb("var2", [R, TILES])
        std2 = sb("std2", [R, TILES])
        rstd2 = sb("rstd2", [R, TILES])
        neg_max = sb("neg_max", [R, GT])
        row_sum = sb("row_sum", [R, GT])
        row_inv = sb("row_inv", [R, GT])
        h_stage = h_all[:, 3 * GT:5 * GT, :].rearrange("p t n -> p (t n)")
        qT = q_pad[:, :, :, :, :].rearrange("p a t b r -> p (a t b r)").rearrange("p (z k w) -> p z k w", z=2, k=KD)
        soft_in = s_sb[:, 0, 0:2, :].rearrange("p a b -> p (a b)")
        probs = s_sb[:, 0, 2:4, :].rearrange("p a b -> p (a b)")
        probsT = s_sb[:, 1, 0:2, :].rearrange("p a b -> p (a b)")
        v2 = v_sb[0:R, 0, :, :]
        out_sb = v_sb[0:R, 1, :, :]

        banks = [ctx.enter_context(nc.psum_tensor(f"bank{i}", [128, 512], f32)) for i in range(8)]
        ring = banks[0:2]
        wo_acc = banks[2:4]
        s_ps = banks[4:6]
        o_ps = banks[6:8]
        hid_ps = banks[2:5]
        down = banks[5:7]
        side = banks[7]

        consts = sem("consts")
        consts2 = sem("consts2")
        pos_ready = sem("pos_ready")
        bias_in = sem("bias_in")
        bias_step = sem("bias_step")
        bias_rows = sem("bias_rows")
        prelude = sem("prelude")
        x_loaded = [sem("x_loaded0"), sem("x_loaded1")]
        staged = [sem(f"staged{i}") for i in range(SLOTS)]
        staged2 = [sem(f"staged2_{i}") for i in range(2)]
        piece_hi = sem("piece_hi")
        piece_lo = sem("piece_lo")
        x_hi = sem("x_hi")
        x_lo = sem("x_lo")
        tok_done = sem("tok_done")
        h_ready = sem("h_ready")
        stat_step = sem("stat_step")
        var_ready = sem("var_ready")
        std_ready = sem("std_ready")
        xn_ready = sem("xn_ready")
        bo_added = sem("bo_added")
        centred = sem("centred")
        t_done = sem("t_done")
        xT_hi = sem("xT_hi")
        xT_lo = sem("xT_lo")
        v_done = sem("v_done")
        v_ready = sem("v_ready")
        q_done = sem("q_done")
        q_ready = sem("q_ready")
        k_done = sem("k_done")
        k_ready = sem("k_ready")
        s_done = sem("s_done")
        s_ready = sem("s_ready")
        o_done = sem("o_done")
        o_hi = sem("o_hi")
        o_lo = sem("o_lo")
        wo_done = sem("wo_done")
        h2_ready = sem("h2_ready")
        var2_ready = sem("var2_ready")
        std2_ready = sem("std2_ready")
        rstd2_ready = sem("rstd2_ready")
        score_done = sem("score_done")
        bits_ready = sem("bits_ready")
        count_done = sem("count_done")
        route_ready = sem("route_ready")
        up_done = sem("up_done")
        hid_hi = sem("hid_hi")
        hid_lo = sem("hid_lo")
        down_done = sem("down_done")
        down_q = sem("down_q")
        down_v = sem("down_v")
        att_done = sem("att_done")
        soft_step = sem("soft_step")
        max_ready = sem("max_ready")
        exp_ready = sem("exp_ready")
        pt_done = sem("pt_done")
        pt_ready = sem("pt_ready")
        av_done = sem("av_done")
        out_ready = sem("out_ready")
        stored = sem("stored")

        def part(base, size, low):
            return arena[:, base + low * size:base + (low + 1) * size]

        def tok_w(k, low):
            return part(WT, KX * D, low)[:, k * D:(k + 1) * D]

        def in_w(base, k, c, n, low):
            at = c // 512 * STAGE + k * 512 + c % 512
            return part(base, KD * INNER, low)[:, at:at + n]

        def out_w(base, c, m, n, low):
            return part(base, CH * D, low)[:, c * D + m:c * D + m + n]

        def piece_dst(i, low):
            _, n, dst, size, off = PIECES[i]
            if dst == NODE_W:
                return node_w[:, low, :, :].rearrange("p k n -> p (k n)")
            return part(dst, size, low)[:, off:off + n]

        def slot(i):
            n = PIECES[i][1]
            if i >= P1_PIECES:
                at, turn = (i - P1_PIECES) % 2, (i - P1_PIECES) // 2 + 1
                return stage[:, at, 0:n], staged2[at], 16 * turn
            at = i % SLOTS
            return ([stage[:, at, 0:n]] if at < 2 else
                    [h_stage[:, (at - 2) * STAGE:(at - 2) * STAGE + n]])[0], staged[at], 16 * (i // SLOTS + 1)

        PRODUCTS = [(0, 0), (0, 1), (1, 0)]

        def tiles_of(g, lo, n):
            return bass.ds(g * GT + lo, n)

        def bank_of(nt, pair):
            return pair if nt == GT else 1

        def for_groups(eng, body):
            body(0, GT, GT)
            with eng.Fori(1, GROUPS - 2) as g:
                body(g, GT, GT)
            body(GROUPS - 2, GT, TAIL)
            body(GROUPS - 1, TAIL, 0)

        block = ctx.enter_context(nc.Block())

        @block.sync
        def _(sp):
            def load_x(g, half):
                sp.dma_start(x_raw[:, 2 * half:2 * half + 2, :],
                             x[tiles_of(g, 2 * half, 2), :, :].rearrange("t p n -> p t n")).then_inc(x_loaded[half], 16)

            def load_piece(i):
                at, n, _, _, _ = PIECES[i]
                dst, arrived, _ = slot(i)
                if i >= SLOTS:
                    sp.wait_ge(piece_lo, i + 1 - SLOTS if i < P1_PIECES else max(P1_PIECES, i - 1))
                sp.dma_start(dst, weights[:, at:at + n]).then_inc(arrived, 16)

            load_piece(0)
            load_x(0, 0)
            load_piece(1)
            load_x(0, 1)
            for i in range(WT_PIECES, SLOTS):
                load_piece(i)
            for dst, src in ((pos_sb, pos), (xn[:, 0, :], tok), (id_sb, ident), (cols_sb, cols)):
                sp.dma_start(dst[:, :], src[:, :]).then_inc(consts, 16)
            for i in range(SLOTS, P1_PIECES):
                load_piece(i)
                if i == SLOTS:
                    for dst, src in ((bo_sb, bo), (bv_sb, bv), (mask_sb, mask), (maskb_sb, mask_bias), (steer_sb, steer)):
                        sp.dma_start(dst[:, :], src[:, :]).then_inc(consts2, 16)

            with sp.Fori(1, GROUPS - 1) as g:
                sp.wait_ge(x_lo, 2 * g)
                load_x(g, 0)
                load_x(g, 1)
            sp.wait_ge(x_lo, 2 * (GROUPS - 1))
            load_x(GROUPS - 1, 0)
            sp.wait_ge(bias_rows, 16 * 3 * TREES)
            for i in range(P1_PIECES, len(PIECES)):
                load_piece(i)

            def store(g, nt):
                sp.wait_ge(out_ready, 2 * g + nt // 2)
                sp.dma_start(out[tiles_of(g, 0, nt), :, :].rearrange("t p n -> p t n"),
                             out_sb[:, 0:nt, :]).then_inc(stored, 16)

            with sp.Fori(0, GROUPS - 1) as g:
                store(g, GT)
            store(GROUPS - 1, TAIL)
            sp.wait_ge(stored, 16 * GROUPS)

        @block.gpsimd
        def _(pool):
            nc.gpsimd.memset(q_pad[:, :, :, :, :], 0.0).then_inc(prelude, 1)

            def split_biases():
                b1_raw = stage[0:TREES, 0, :]
                b2_raw = stage[:, 1, 0:TREES * D]
                b1_parts = [stage[0:TREES, 1, 0:HID // 2].bitcast(bf16), stage[0:TREES, 1, HID // 2:HID].bitcast(bf16)]
                pool.wait_ge(piece_lo, P1_PIECES)
                pool.dma_start(b1_raw, b1[:, :]).then_inc(bias_in, 16)
                pool.dma_start(b2_raw, b2[:, :]).then_inc(bias_in, 16)
                pool.dma_start(e_sb[:, :, :].rearrange("p t n -> p (t n)"), e_mask[:, :]).then_inc(bias_in, 16)
                pool.wait_ge(bias_in, 48)
                b2_all = b2_sb[:, :, :].rearrange("p t n -> p (t n)")
                low = slice(SEL_ROWS[1], 128)
                nc.gpsimd.tensor_copy(b2_all, b2_raw).then_inc(bias_step, 1)
                pool.wait_ge(bias_step, 1)
                nc.gpsimd.tensor_tensor(b2_all[low, :], b2_raw[low, :], b2_all[low, :].bitcast(f32),
                                        ALU.subtract).then_inc(bias_step, 1)
                pool.wait_ge(bias_step, 2)
                for i in range(3):
                    piece = b1_parts[i % 2]
                    if i == 2:
                        pool.wait_ge(bias_rows, 32 * TREES)
                    nc.gpsimd.tensor_copy(piece, b1_raw).then_inc(bias_step, 1)
                    pool.wait_ge(bias_step, 2 * i + 3)
                    for t in range(TREES):
                        pool.dma_start(e_sb[ONE_ROW + i:ONE_ROW + i + 1, t, :], piece[t:t + 1, :]).then_inc(bias_rows, 16)
                    if i < 2:
                        nc.gpsimd.tensor_tensor(b1_raw, b1_raw, piece, ALU.subtract).then_inc(bias_step, 1)
                        pool.wait_ge(bias_step, 2 * i + 4)

            pool.wait_ge(consts2, 16 * CONSTS2)

            def add_bo(g, nt):
                pool.wait_ge(xn_ready, g + 1)
                h = h_all[0:R, tiles_of(g, 0, nt), :]
                nc.gpsimd.tensor_tensor(h, h, bo_sb[:, :].unsqueeze(1).to_broadcast([R, nt, D]), ALU.add).then_inc(bo_added, 1)

            def x_split_lo(g, half):
                pool.wait_ge(x_hi, 2 * g + half + 1)
                n = 2 * KX * R
                nc.gpsimd.tensor_tensor(arena[:, XLO + half * n:XLO + (half + 1) * n],
                                        x_raw[:, 2 * half:2 * half + 2, :].rearrange("p t n -> p (t n)"),
                                        arena[:, XHI + half * n:XHI + (half + 1) * n].bitcast(f32),
                                        ALU.subtract).then_inc(x_lo, 1)

            add_bo(0, GT)
            x_split_lo(1, 0)
            x_split_lo(1, 1)
            split_biases()
            add_bo(1, GT)
            with pool.Fori(2, GROUPS - 1) as g:
                x_split_lo(g, 0)
                x_split_lo(g, 1)
                add_bo(g, GT)
            x_split_lo(GROUPS - 1, 0)
            add_bo(GROUPS - 1, TAIL)

            def split_piece(i):
                src, arrived, value = slot(i)
                pool.wait_ge(arrived, value)
                nc.gpsimd.tensor_copy(piece_dst(i, 0), src).then_inc(piece_hi, 1)
                pool.wait_ge(piece_hi, i + 1)
                nc.gpsimd.tensor_tensor(piece_dst(i, 1), src, piece_dst(i, 0).bitcast(f32), ALU.subtract).then_inc(piece_lo, 1)

            def normalise(g, nt):
                pool.wait_ge(rstd2_ready, g + 1)
                pool.wait_ge(t_done, KD * (GROUPS + g))
                cut = tiles_of(g, 0, nt)
                nc.gpsimd.tensor_tensor(xn[:, 0:nt, :], h_all[0:R, cut, :], mean2[:, cut].unsqueeze(2).to_broadcast([R, nt, D]),
                                        ALU.subtract).then_inc(centred, 1)
                pool.wait_ge(centred, g + 1)
                nc.gpsimd.tensor_tensor(xn[:, 0:nt, :], xn[:, 0:nt, :], rstd2[:, cut].unsqueeze(2).to_broadcast([R, nt, D]),
                                        ALU.mult).then_inc(xn_ready, 1)

            normalise(0, GT)
            per = 2
            at = P1_PIECES
            pool.wait_ge(tok_done, 2 * (GROUPS - 1) + TAIL // 2)
            for i in range(at, at + 2 * per):
                split_piece(i)
            pool.wait_ge(q_done, PAIRS * GROUPS)
            pool.wait_ge(k_done, PAIRS * GROUPS)
            for i in range(at + 2 * per, at + 5 * per):
                split_piece(i)
            pool.wait_ge(wo_done, PAIRS * GROUPS)
            for i in range(at + 5 * per, at + 6 * per):
                split_piece(i)
            with pool.Fori(1, GROUPS - 1) as g:
                normalise(g, GT)
            normalise(GROUPS - 1, TAIL)

        @block.scalar
        def _(act):
            def split_hi(i):
                src, arrived, value = slot(i)
                act.wait_ge(arrived, value)
                nc.scalar.activation(piece_dst(i, 0), src, ACT.Copy).then_inc(piece_hi, 1)

            def x_split_hi(g, half):
                act.wait_ge(x_loaded[half], 16 * (g + 1))
                if not first_group(g):
                    act.wait_ge(tok_done, 2 * g)
                n = 2 * KX * R
                nc.scalar.activation(arena[:, XHI + half * n:XHI + (half + 1) * n],
                                     x_raw[:, 2 * half:2 * half + 2, :].rearrange("p t n -> p (t n)"),
                                     ACT.Copy).then_inc(x_hi, 1)

            def root(g, nt):
                act.wait_ge(var_ready, g + 1)
                nc.scalar.activation(std[:, 0:nt], mv[:, 0:nt, 1], ACT.Sqrt).then_inc(std_ready, 1)

            def transposed_hi(n, nt):
                for k in range(KD):
                    act.wait_ge(t_done, KD * n + k + 1)
                    nc.scalar.activation(xT[:, 0, k, 0:nt * R], ring[k][:, 0:nt * R], ACT.Copy).then_inc(xT_hi, 1)

            def q_evac(g, nt, j):
                act.wait_ge(q_done, PAIRS * g + j + 1)
                if j >= 2:
                    act.wait_ge(s_done, 2 * PAIRS * g + nt // 2 * (j - 1))
                for half in range(2):
                    rows = slice(HD * half, HD * (half + 1))
                    last = nc.scalar.activation(q_pad[rows, j % 2, 0:nt, half, :],
                                                ring[0][rows, 0:nt * R].rearrange("p (t r) -> p t r", r=R),
                                                ACT.Identity, bias=cols_sb[rows, j:j + 1])
                last.then_inc(q_ready, 1)

            def o_evac_hi(g, nt, j):
                if j >= 2:
                    act.wait_ge(wo_done, PAIRS * g + j - 1)
                for tp in range(nt // 2):
                    act.wait_ge(o_done, 2 * PAIRS * g + nt // 2 * j + tp + 1)
                    for half in range(2):
                        rows = slice(HD * half, HD * (half + 1))
                        src = o_ps[tp][rows, 0:2 * HW].rearrange("p (t h r) -> p t h r", t=2, h=2)
                        last = nc.scalar.activation(
                            pairT[rows, j % 2, 0, tp * HW:(tp + 1) * HW].rearrange("p (t r) -> p t r", r=R),
                            src[:, :, half, :], ACT.Copy)
                    last.then_inc(o_hi, 1)

            for i in (0, 1):
                split_hi(i)
                x_split_hi(0, i)
            for i in range(2, 6):
                split_hi(i)
            root(0, GT)
            transposed_hi(0, GT)
            for i in range(6, P1_PIECES):
                split_hi(i)

            def attention(g, nt, nxt):
                for j in range(PAIRS + 3):
                    if j < PAIRS:
                        q_evac(g, nt, j)
                    if j in (1, 2) and 2 * (j - 1) < nxt:
                        x_split_hi(g + 1, j - 1)
                    if j == 3 and not first_group(g):
                        root2(g - 1, GT)
                    if j == 6 and nxt:
                        root(g + 1, nxt)
                    if j == 8:
                        transposed_hi(g + 1, nxt or GT)
                    if 2 <= j < PAIRS + 2:
                        o_evac_hi(g, nt, j - 2)

            def root2(g, nt):
                act.wait_ge(var2_ready, g + 1)
                nc.scalar.activation(std2[:, tiles_of(g, 0, nt)], var2[:, tiles_of(g, 0, nt)], ACT.Sqrt).then_inc(std2_ready, 1)

            for_groups(act, attention)
            root2(GROUPS - 1, TAIL)

            def hidden_hi(g, nt, s):
                act.wait_ge(up_done, 3 * CH * g + s + 1)
                if s >= 3:
                    act.wait_ge(down_done, 3 * CH * g + s - 2)
                nc.scalar.activation(pairT[:, s % 3, 0, 0:nt * R], hid_ps[s % 3][:, 0:nt * R], ACT.Relu).then_inc(hid_hi, 1)

            def probs_out(g, nt):
                act.wait_ge(pt_done, g + 1)
                nc.scalar.activation(probsT[:, 0:nt * R], ring[1][0:R, 0:nt * R], ACT.Copy).then_inc(pt_ready, 1)

            def ffn(g, nt, nxt, first=False):
                for s in range(TREES * CH + 2):
                    if s < TREES * CH:
                        hidden_hi(g, nt, s)
                    for tree in range(2):
                        if s == CH * (tree + 1) + 1:
                            act.wait_ge(down_done, 3 * CH * g + CH * (tree + 1))
                            for m in range(KD):
                                last = nc.scalar.activation(qT[:, tree, m, 0:nt * R], down[m][:, 0:nt * R], ACT.Copy)
                            last.then_inc(down_q, 1)
                    if s == 2 and not first:
                        exps(g - 1, GT)
                    if s == 5 and not first:
                        probs_out(g - 1, GT)
                    if s == TREES * CH and nxt:
                        transposed_hi(GROUPS + g + 1, nxt)

            def exps(g, nt):
                act.wait_ge(max_ready, g + 1)
                for t in range(nt):
                    last = nc.scalar.activation(probs[:, t * R:(t + 1) * R], soft_in[:, t * R:(t + 1) * R], ACT.Exp,
                                                bias=neg_max[:, t:t + 1], accum_out=row_sum[:, t:t + 1])
                last.then_inc(exp_ready, 1)

            ffn(0, GT, GT, first=True)
            with act.Fori(1, GROUPS - 2) as g:
                ffn(g, GT, GT)
            ffn(GROUPS - 2, GT, TAIL)
            ffn(GROUPS - 1, TAIL, 0)
            exps(GROUPS - 1, TAIL)
            probs_out(GROUPS - 1, TAIL)

        @block.vector
        def _(dve):
            def split_lo(i):
                src, _, _ = slot(i)
                dve.wait_ge(piece_hi, i + 1)
                nc.vector.tensor_tensor(piece_dst(i, 1), src, piece_dst(i, 0).bitcast(f32),
                                        ALU.subtract).then_inc(piece_lo, 1)

            def x_split_lo(g, half):
                dve.wait_ge(x_hi, 2 * g + half + 1)
                n = 2 * KX * R
                nc.vector.tensor_tensor(arena[:, XLO + half * n:XLO + (half + 1) * n],
                                        x_raw[:, 2 * half:2 * half + 2, :].rearrange("p t n -> p (t n)"),
                                        arena[:, XHI + half * n:XHI + (half + 1) * n].bitcast(f32),
                                        ALU.subtract).then_inc(x_lo, 1)

            def embed(g, nt):
                for tp in range(nt // 2):
                    dve.wait_ge(tok_done, 2 * g + tp + 1)
                    nc.vector.tensor_tensor(h_all[0:R, tiles_of(g, 2 * tp, 2), :],
                                            ring[bank_of(nt, tp)][0:R, :].rearrange("p (t n) -> p t n", t=2),
                                            pos_sb[:, :].unsqueeze(1).to_broadcast([R, 2, D]), ALU.add).then_inc(h_ready, 1)

            def moments(g, nt):
                base = 0 if first_group(g) else 5 * g - 2
                dve.wait_ge(h_ready, 2 * g + nt // 2)
                nc.vector.memset(bearer[:, 0:1], 0.0)
                for t in range(nt):
                    last = nc.vector.bn_stats(stats[:, t, :], h_all[0:R, tiles_of(g, t, 1), :].rearrange("p t n -> p (t n)"))
                last.then_inc(stat_step, 1)
                dve.wait_ge(stat_step, base + 1)
                nc.vector.memset(bearer[:, 1:2], 0.0)
                for t in range(nt):
                    last = nc.vector.bn_aggr(mv[:, t, :], stats[:, t, :])
                last.then_inc(stat_step, 1)
                dve.wait_ge(stat_step, base + 2)
                nc.vector.tensor_scalar(mv[:, 0:nt, 1], mv[:, 0:nt, 1], EPS, None, ALU.add).then_inc(var_ready, 1)

            def normalise(g, nt):
                dve.wait_ge(std_ready, g + 1)
                nc.vector.reciprocal(rstd[:, 0:nt], std[:, 0:nt]).then_inc(stat_step, 1)
                dve.wait_ge(stat_step, 3 if first_group(g) else 5 * g + 1)
                if not first_group(g):
                    dve.wait_ge(t_done, KD * g)
                for t in range(nt):
                    last = nc.vector.tensor_scalar(xn[:, t, :], h_all[0:R, tiles_of(g, t, 1), :].rearrange("p t n -> p (t n)"),
                                                   mv[:, t, 0:1], rstd[:, t:t + 1], ALU.subtract, ALU.mult)
                last.then_inc(xn_ready, 1)

            def transposed_lo(n, nt):
                for k in range(KD):
                    dve.wait_ge(xT_hi, KD * n + k + 1)
                    nc.vector.tensor_tensor(xT[:, 1, k, 0:nt * R], ring[k][:, 0:nt * R],
                                            xT[:, 0, k, 0:nt * R].bitcast(f32), ALU.subtract).then_inc(xT_lo, 1)

            def v_evac(g, nt, quarter):
                if quarter >= 2:
                    dve.wait_ge(o_done, 2 * PAIRS * g + nt // 2 * (2 * quarter - 2))
                for tp in range(nt // 2):
                    dve.wait_ge(v_done, PAIRS * g + nt // 2 * quarter + tp + 1)
                    nc.vector.tensor_tensor(v_sb[0:R, quarter % 2, 2 * tp:2 * tp + 2, :],
                                            ring[bank_of(nt, tp)][0:R, :].rearrange("p (t n) -> p t n", t=2),
                                            bv_sb[:, quarter * D:(quarter + 1) * D].unsqueeze(1).to_broadcast([R, 2, D]),
                                            ALU.add).then_inc(v_ready, 1)

            def k_evac(g, nt, j):
                dve.wait_ge(k_done, PAIRS * g + j + 1)
                if j >= 2:
                    dve.wait_ge(s_done, 2 * PAIRS * g + nt // 2 * (j - 1))
                nc.vector.tensor_scalar(k_sb[:, j % 2, 0:nt * R], ring[1][:, 0:nt * R], cols_sb[:, PAIRS + j:PAIRS + j + 1],
                                        None, ALU.add).then_inc(k_ready, 1)

            def s_evac(g, nt, j):
                if j >= 2:
                    dve.wait_ge(o_done, 2 * PAIRS * g + nt // 2 * (j - 1))
                for tp in range(nt // 2):
                    dve.wait_ge(s_done, 2 * PAIRS * g + nt // 2 * j + tp + 1)
                    nc.vector.tensor_tensor(s_sb[:, j % 2, 2 * tp:2 * tp + 2, :].rearrange("p t (h r) -> p (t h) r", h=2),
                                            s_ps[tp][0:R, 0:2 * HW].rearrange("p (b r) -> p b r", r=R),
                                            mask_sb[:, :].unsqueeze(1).to_broadcast([R, 4, R]), ALU.mult).then_inc(s_ready, 1)

            def o_evac_lo(g, nt, j):
                for tp in range(nt // 2):
                    dve.wait_ge(o_hi, 2 * PAIRS * g + nt // 2 * j + tp + 1)
                    for half in range(2):
                        rows = slice(HD * half, HD * (half + 1))
                        src = o_ps[tp][rows, 0:2 * HW].rearrange("p (t h r) -> p t h r", t=2, h=2)
                        cut = slice(tp * HW, (tp + 1) * HW)
                        last = nc.vector.tensor_tensor(
                            pairT[rows, j % 2, 1, cut].rearrange("p (t r) -> p t r", r=R), src[:, :, half, :],
                            pairT[rows, j % 2, 0, cut].bitcast(f32).rearrange("p (t r) -> p t r", r=R), ALU.subtract)
                    last.then_inc(o_lo, 1)

            def residual(g, nt):
                dve.wait_ge(wo_done, PAIRS * (g + 1))
                dve.wait_ge(bo_added, g + 1)
                for tp in range(nt // 2):
                    h = h_all[0:R, tiles_of(g, 2 * tp, 2), :]
                    nc.vector.tensor_tensor(h, wo_acc[tp][0:R, :].rearrange("p (t n) -> p t n", t=2), h, ALU.add).then_inc(h2_ready, 1)

            def moments2(g, nt):
                dve.wait_ge(h2_ready, 2 * g + nt // 2)
                nc.vector.memset(bearer[:, 0:1], 0.0)
                for t in range(nt):
                    last = nc.vector.bn_stats(stats[:, t, :], h_all[0:R, tiles_of(g, t, 1), :].rearrange("p t n -> p (t n)"))
                last.then_inc(stat_step, 1)
                base = 5 * g + (6 if nt == GT else 3)
                dve.wait_ge(stat_step, base + 1)
                nc.vector.memset(bearer[:, 1:2], 0.0)
                for t in range(nt):
                    last = nc.vector.bn_aggr(mv[:, t, :], stats[:, t, :])
                last.then_inc(stat_step, 1)
                dve.wait_ge(stat_step, base + 2)
                nc.vector.tensor_copy(mean2[:, tiles_of(g, 0, nt)], mv[:, 0:nt, 0])
                nc.vector.tensor_scalar(var2[:, tiles_of(g, 0, nt)], mv[:, 0:nt, 1], EPS, None, ALU.add).then_inc(var2_ready, 1)

            def invert2(g, nt):
                dve.wait_ge(std2_ready, g + 1)
                nc.vector.reciprocal(rstd2[:, tiles_of(g, 0, nt)], std2[:, tiles_of(g, 0, nt)]).then_inc(rstd2_ready, 1)

            for i in (0, 1):
                split_lo(i)
                x_split_lo(0, i)
            for i in (2, 3):
                split_lo(i)
            dve.wait_ge(consts, 16 * CONSTS)
            nc.vector.tensor_tensor(pos_sb[:, :], pos_sb[:, :], xn[:, 0, :], ALU.add).then_inc(pos_ready, 1)
            dve.wait_ge(pos_ready, 1)
            embed(0, GT)
            moments(0, GT)
            for i in (4, 5):
                split_lo(i)
            normalise(0, GT)
            transposed_lo(0, GT)
            for i in range(6, P1_PIECES):
                split_lo(i)
            dve.wait_ge(consts2, 16 * CONSTS2)

            def attention(g, nt, nxt):
                for j in range(PAIRS + 3):
                    if j < PAIRS:
                        if j % 2 == 0:
                            v_evac(g, nt, j // 2)
                        if j == 5 and nxt:
                            embed(g + 1, nxt)
                        k_evac(g, nt, j)
                    if j == 0 and not first_group(g):
                        residual(g - 1, GT)
                    if j == 2 and not first_group(g):
                        moments2(g - 1, GT)
                    if j == 4 and not first_group(g):
                        invert2(g - 1, GT)
                    if j == 8:
                        transposed_lo(g + 1, nxt or GT)
                    if 1 <= j < PAIRS + 1:
                        s_evac(g, nt, j - 1)
                    if 2 <= j < PAIRS + 2:
                        o_evac_lo(g, nt, j - 2)
                    if j == 5 and nxt:
                        moments(g + 1, nxt)
                    if j == 6 and nxt:
                        normalise(g + 1, nxt)

            for_groups(dve, attention)
            residual(GROUPS - 1, TAIL)
            moments2(GROUPS - 1, TAIL)
            invert2(GROUPS - 1, TAIL)

            def route_bits(g, nt):
                dve.wait_ge(score_done, g + 1)
                nc.vector.tensor_scalar(bitsT[:, 0:nt * R], side[:, 0:nt * R], cols_sb[:, 2 * PAIRS:2 * PAIRS + 1], 0.0,
                                        ALU.add, ALU.is_ge).then_inc(bits_ready, 1)

            def route(g, nt):
                for n, (dst, src) in enumerate(((routeT, ring[1]), (selT, side))):
                    dve.wait_ge(count_done, 2 * g + n + 1)
                    nc.vector.tensor_scalar(dst[:, 0:nt * R], src[:, 0:nt * R], cols_sb[:, 2 * PAIRS + 1 + n:2 * PAIRS + 2 + n],
                                            None, ALU.is_ge).then_inc(route_ready, 1)

            def hidden_lo(g, nt, s):
                dve.wait_ge(hid_hi, 3 * CH * g + s + 1)
                nc.vector.scalar_tensor_tensor(pairT[:, s % 3, 1, 0:nt * R], hid_ps[s % 3][:, 0:nt * R], 0.0,
                                               pairT[:, s % 3, 0, 0:nt * R].bitcast(f32), ALU.max, ALU.subtract).then_inc(hid_lo, 1)

            def softmax_in(g, nt):
                dve.wait_ge(att_done, g + 1)
                nc.vector.scalar_tensor_tensor(soft_in[:, 0:nt * R].rearrange("p (t r) -> p t r", r=R),
                                               ring[0][0:R, 0:nt * R].rearrange("p (t r) -> p t r", r=R), float(D) ** -0.5,
                                               maskb_sb[:, :].unsqueeze(1).to_broadcast([R, nt, R]),
                                               ALU.mult, ALU.add).then_inc(soft_step, 1)
                dve.wait_ge(soft_step, 3 * g + 1)
                nc.vector.tensor_reduce(row_inv[:, 0:nt], soft_in[:, 0:nt * R].rearrange("p (t r) -> p t r", r=R),
                                        AX.X, ALU.max).then_inc(soft_step, 1)
                dve.wait_ge(soft_step, 3 * g + 2)
                nc.vector.tensor_scalar(neg_max[:, 0:nt], row_inv[:, 0:nt], -1.0, None, ALU.mult).then_inc(max_ready, 1)

            def finish(g, nt):
                dve.wait_ge(exp_ready, g + 1)
                nc.vector.reciprocal(row_inv[:, 0:nt], row_sum[:, 0:nt]).then_inc(soft_step, 1)
                dve.wait_ge(soft_step, 3 * g + 3)
                if not first_group(g):
                    dve.wait_ge(stored, 16 * g)
                for tp in range(nt // 2):
                    dve.wait_ge(av_done, 2 * g + tp + 1)
                    for t in (2 * tp, 2 * tp + 1):
                        last = nc.vector.scalar_tensor_tensor(out_sb[:, t, :], ring[tp][0:R, t % 2 * D:(t % 2 + 1) * D],
                                                              row_inv[:, t:t + 1],
                                                              h_all[0:R, tiles_of(g, t, 1), :].rearrange("p t n -> p (t n)"),
                                                              ALU.mult, ALU.add)
                    last.then_inc(out_ready, 1)

            route_bits(0, GT)
            route(0, GT)

            def ffn(g, nt, nxt, first=False):
                for s in range(TREES * CH + 2):
                    if s < TREES * CH:
                        hidden_lo(g, nt, s)
                    if s == 1 and not first:
                        softmax_in(g - 1, GT)
                    if s == 7 and not first:
                        finish(g - 1, GT)
                    if s == TREES * CH and nxt:
                        transposed_lo(GROUPS + g + 1, nxt)
                dve.wait_ge(down_done, 3 * CH * (g + 1))
                for tp in range(nt // 2):
                    last = nc.vector.tensor_copy(v2[:, 2 * tp:2 * tp + 2, :], down[tp][0:R, :].rearrange("p (t n) -> p t n", t=2))
                last.then_inc(down_v, 1)
                if nxt:
                    route_bits(g + 1, nxt)
                    route(g + 1, nxt)

            ffn(0, GT, GT, first=True)
            with dve.Fori(1, GROUPS - 2) as g:
                ffn(g, GT, GT)
            ffn(GROUPS - 2, GT, TAIL)
            ffn(GROUPS - 1, TAIL, 0)
            softmax_in(GROUPS - 1, TAIL)
            finish(GROUPS - 1, TAIL)

        @block.tensor
        def _(pe):
            def embed(g, nt):
                for t in range(nt):
                    if t % 2 == 0:
                        pe.wait_ge(x_lo, 2 * g + t // 2 + 1)
                    for k in range(KX):
                        for n, (a, b) in enumerate(PRODUCTS):
                            at = (XLO if a else XHI) + t * KX * R + k * R
                            last = nc.tensor.matmul(ring[bank_of(nt, t // 2)][0:R, t % 2 * D:(t % 2 + 1) * D], arena[:, at:at + R],
                                                    tok_w(k, b), start=(k == n == 0), stop=(k == KX - 1 and n == 2),
                                                    skip_group_check=True)
                    if t % 2:
                        last.then_inc(tok_done, 1)

            def turn(n, nt):
                pe.wait_ge(xn_ready, n + 1)
                for k in range(KD):
                    for t in range(nt):
                        last = nc.tensor.transpose(ring[k][:, t * R:(t + 1) * R], xn[:, t, k * 128:(k + 1) * 128],
                                                   id_sb[0:R, 0:R])
                    last.then_inc(t_done, 1)

            def values(g, nt, quarter):
                if quarter == 0:
                    pe.wait_ge(xT_lo, KD * (g + 1))
                for t in range(nt):
                    bank = bank_of(nt, t // 2)
                    if t % 2 == 0 and quarter:
                        pe.wait_ge(k_ready if bank else q_ready, PAIRS * g + 2 * quarter)
                    n = 0
                    for k in range(KD):
                        for a, b in PRODUCTS:
                            last = nc.tensor.matmul(ring[bank][0:R, t % 2 * D:(t % 2 + 1) * D],
                                                    xT[:, a, k, t * R:(t + 1) * R], in_w(WV, k, quarter * D, D, b),
                                                    start=(n == 0), stop=(n == 5), skip_group_check=True)
                            n += 1
                    if t % 2:
                        last.then_inc(v_done, 1)

            def project(g, nt, j, bank, base, done):
                n = 0
                for k in range(KD):
                    for a, b in PRODUCTS:
                        last = nc.tensor.matmul(ring[bank][:, 0:nt * R], in_w(base, k, 128 * j, 128, a),
                                                xT[:, b, k, 0:nt * R], start=(n == 0), stop=(n == 5))
                        n += 1
                last.then_inc(done, 1)

            def scores(g, nt, j):
                pe.wait_ge(q_ready, PAIRS * g + j + 1)
                pe.wait_ge(k_ready, PAIRS * g + j + 1)
                for t in range(nt):
                    if t % 2 == 0:
                        if j:
                            pe.wait_ge(s_ready, 2 * PAIRS * g + nt // 2 * (j - 1) + t // 2 + 1)
                    last = nc.tensor.matmul(s_ps[t // 2][0:R, t % 2 * 2 * R:(t % 2 + 1) * 2 * R],
                                            k_sb[:, j % 2, t * R:(t + 1) * R],
                                            q_pad[:, j % 2, t, :, :].rearrange("p h r -> p (h r)"),
                                            start=True, stop=True, skip_group_check=True)
                    if t % 2:
                        last.then_inc(s_done, 1)

            def mix(g, nt, j):
                pe.wait_ge(v_ready, PAIRS * g + nt // 2 * (j // 2 + 1))
                for t in range(nt):
                    if t % 2 == 0:
                        pe.wait_ge(s_ready, 2 * PAIRS * g + nt // 2 * j + t // 2 + 1)
                        if j:
                            pe.wait_ge(o_lo, 2 * PAIRS * g + nt // 2 * (j - 1) + t // 2 + 1)
                    last = nc.tensor.matmul(o_ps[t // 2][:, t % 2 * 2 * R:(t % 2 + 1) * 2 * R],
                                            v_sb[0:R, j // 2 % 2, t, j % 2 * 128:(j % 2 + 1) * 128],
                                            s_sb[:, j % 2, t, :], start=True, stop=True, skip_group_check=True)
                    if t % 2:
                        last.then_inc(o_done, 1)

            def project_out(g, nt, j):
                pe.wait_ge(o_lo, 2 * PAIRS * g + nt // 2 * (j + 1))
                if j == 0 and not first_group(g):
                    pe.wait_ge(h2_ready, 2 * g)
                for t in range(nt):
                    for n, (a, b) in enumerate(PRODUCTS):
                        last = nc.tensor.matmul(wo_acc[t // 2][0:R, t % 2 * D:(t % 2 + 1) * D],
                                                pairT[:, j % 2, a, t * R:(t + 1) * R], out_w(WO, j, 0, D, b),
                                                start=(j == 0 and n == 0 and t % 2 == 0),
                                                stop=(j == PAIRS - 1 and n == 2), skip_group_check=True)
                last.then_inc(wo_done, 1)

            def node_scores(g, nt):
                pe.wait_ge(xT_lo, KD * (GROUPS + g + 1))
                n = 0
                for k in range(KD):
                    for a, b in PRODUCTS:
                        last = nc.tensor.matmul(side[:, 0:nt * R], node_w[:, a, k, :], xT[:, b, k, 0:nt * R],
                                                start=(n == 0), stop=(n == 5))
                        n += 1
                last.then_inc(score_done, 1)

            def path_counts(g, nt):
                pe.wait_ge(bits_ready, g + 1)
                nc.tensor.matmul(ring[1][:, 0:nt * R], steer_sb[:, 0:128], bitsT[:, 0:nt * R],
                                 start=True, stop=True).then_inc(count_done, 1)
                nc.tensor.matmul(side[:, 0:nt * R], steer_sb[:, 128:256], bitsT[:, 0:nt * R],
                                 start=True, stop=True).then_inc(count_done, 1)

            pe.wait_ge(piece_lo, WT_PIECES)
            embed(0, GT)
            pe.wait_ge(consts, 16 * CONSTS)
            turn(0, GT)
            pe.wait_ge(prelude, 1)

            def attention(g, nt, nxt):
                for j in range(PAIRS + 3):
                    if first_group(g) and j in (0, PAIRS // 2):
                        pe.wait_ge(piece_lo, WT_PIECES + (HALF_PIECES if j else 0) + 3)
                    if first_group(g) and j in (3, 3 + PAIRS // 2):
                        pe.wait_ge(piece_lo, WT_PIECES + (HALF_PIECES if j > 3 else 0) + 4)
                    if j < PAIRS:
                        if j % 2 == 0:
                            values(g, nt, j // 2)
                        if j == 5 and nxt:
                            pe.wait_ge(q_ready, PAIRS * g + j)
                            pe.wait_ge(k_ready, PAIRS * g + j)
                            embed(g + 1, nxt)
                        if j % 2 == 0 and nt == GT:
                            pe.wait_ge(v_ready, PAIRS * g + j + 1)
                        elif j == 5 and nxt == GT:
                            pe.wait_ge(h_ready, 2 * (g + 1) + 1)
                        elif j:
                            pe.wait_ge(q_ready, PAIRS * g + j)
                        project(g, nt, j, 0, WQ, q_done)
                        if j % 2 == 0:
                            pe.wait_ge(v_ready, PAIRS * g + nt // 2 * (j // 2 + 1))
                        elif j == 5 and nxt:
                            pe.wait_ge(h_ready, 2 * (g + 1) + nxt // 2)
                        else:
                            pe.wait_ge(k_ready, PAIRS * g + j)
                        project(g, nt, j, 1, WK, k_done)
                    if j == 8:
                        pe.wait_ge(q_ready, PAIRS * (g + 1))
                        pe.wait_ge(k_ready, PAIRS * (g + 1))
                        turn(g + 1, nxt or GT)
                    if 1 <= j < PAIRS + 1:
                        scores(g, nt, j - 1)
                    if 2 <= j < PAIRS + 2:
                        mix(g, nt, j - 2)
                    if j >= 3:
                        project_out(g, nt, j - 3)

            for_groups(pe, attention)

            pe.wait_ge(h2_ready, 2 * (GROUPS - 1) + TAIL // 2)

            def up(g, nt, s):
                tree, c = s // CH, s % CH
                if s >= 3:
                    pe.wait_ge(hid_lo, 3 * CH * g + s - 2)
                elif not first_group(g):
                    pe.wait_ge(hid_lo, 3 * CH * g)
                n = 0
                for k in range(KD):
                    for a, b in PRODUCTS:
                        nc.tensor.matmul(hid_ps[s % 3][:, 0:nt * R], in_w(W1[tree], k, 128 * c, 128, a),
                                         xT[:, b, k, 0:nt * R], start=(n == 0), stop=False)
                        n += 1
                if s == 0:
                    pe.wait_ge(route_ready, 2 * g + 2)
                nc.tensor.matmul(hid_ps[s % 3][:, 0:nt * R], e_sb[:, tree, 128 * c:128 * (c + 1)], routeT[:, 0:nt * R],
                                 start=False, stop=True).then_inc(up_done, 1)

            def down_step(g, nt, s):
                tree, c = s // CH, s % CH
                pe.wait_ge(hid_lo, 3 * CH * g + s + 1)
                if c == 0 and tree:
                    pe.wait_ge(down_q, 2 * g + tree)
                elif c == 0 and not first_group(g):
                    pe.wait_ge(down_v, g)
                if tree < 2:
                    for m in range(KD):
                        for n, (a, b) in enumerate(PRODUCTS):
                            last = nc.tensor.matmul(down[m][:, 0:nt * R], out_w(W2[tree], c, 128 * m, 128, a),
                                                    pairT[:, s % 3, b, 0:nt * R], start=(c == n == 0), stop=False,
                                                    skip_group_check=True)
                        if c == CH - 1:
                            last = nc.tensor.matmul(down[m][:, 0:nt * R], b2_sb[:, tree, 128 * m:128 * (m + 1)],
                                                    selT[:, 0:nt * R], start=False, stop=True, skip_group_check=True)
                else:
                    for t in range(nt):
                        acc = down[t // 2][0:R, t % 2 * D:(t % 2 + 1) * D]
                        for n, (a, b) in enumerate(PRODUCTS):
                            last = nc.tensor.matmul(acc, pairT[:, s % 3, a, t * R:(t + 1) * R], out_w(W2[tree], c, 0, D, b),
                                                    start=(c == n == 0 and t % 2 == 0), stop=False, skip_group_check=True)
                        if c == CH - 1:
                            last = nc.tensor.matmul(acc, selT[:, t * R:(t + 1) * R], b2_sb[:, tree, :],
                                                    start=False, stop=True, skip_group_check=True)
                last.then_inc(down_done, 1)

            def attend(g, nt):
                pe.wait_ge(down_q, 2 * (g + 1))
                for t in range(nt):
                    for k in range(KD):
                        last = nc.tensor.matmul(ring[0][0:R, t * R:(t + 1) * R], qT[:, 0, k, t * R:(t + 1) * R],
                                                qT[:, 1, k, t * R:(t + 1) * R], start=(k == 0), stop=(k == KD - 1),
                                                skip_group_check=True)
                last.then_inc(att_done, 1)

            def turn_probs(g, nt):
                pe.wait_ge(exp_ready, g + 1)
                for t in range(nt):
                    last = nc.tensor.transpose(ring[1][0:R, t * R:(t + 1) * R], probs[:, t * R:(t + 1) * R], id_sb[0:R, 0:R])
                last.then_inc(pt_done, 1)

            def weigh(g, nt):
                pe.wait_ge(pt_ready, g + 1)
                pe.wait_ge(down_v, g + 1)
                for t in range(nt):
                    last = nc.tensor.matmul(ring[t // 2][0:R, t % 2 * D:(t % 2 + 1) * D], probsT[:, t * R:(t + 1) * R],
                                            v2[:, t, :], start=True, stop=True, skip_group_check=True)
                    if t % 2:
                        last.then_inc(av_done, 1)

            pe.wait_ge(piece_lo, P1_PIECES)
            node_scores(0, GT)
            path_counts(0, GT)
            pe.wait_ge(bias_rows, 16 * 3 * TREES)

            def ffn(g, nt, nxt, first=False):
                for s in range(TREES * CH + 2):
                    if first and s % CH == 0 and s < TREES * CH:
                        pe.wait_ge(piece_lo, P1_PIECES + (s // CH) * 4 + 2)
                    if first and s % CH == 2 and s < TREES * CH:
                        pe.wait_ge(piece_lo, P1_PIECES + (s // CH) * 4 + 4)
                    if s < TREES * CH:
                        up(g, nt, s)
                    if s == 5 and not first:
                        pe.wait_ge(route_ready, 2 * g + 2)
                        turn_probs(g - 1, GT)
                    if s == 7 and not first:
                        weigh(g - 1, GT)
                    if s == TREES * CH and nxt:
                        if not first:
                            pe.wait_ge(out_ready, 2 * g)
                        turn(GROUPS + g + 1, nxt)
                    if s >= 2:
                        down_step(g, nt, s - 2)
                if nxt:
                    node_scores(g + 1, nxt)
                elif not first:
                    pe.wait_ge(out_ready, 2 * g)
                attend(g, nt)
                if nxt:
                    path_counts(g + 1, nxt)

            ffn(0, GT, GT, first=True)
            with pe.Fori(1, GROUPS - 2) as g:
                ffn(g, GT, GT)
            ffn(GROUPS - 2, GT, TAIL)
            ffn(GROUPS - 1, TAIL, 0)
            turn_probs(GROUPS - 1, TAIL)
            weigh(GROUPS - 1, TAIL)


def launch_arrays(i):
    f = np.float32
    x = np.zeros((TILES * PER_TILE,) + i["x"].shape[1:], f)
    x[:IMAGES] = i["x"]
    n = SIDE // PATCH
    x = x.reshape(TILES, PER_TILE, CHANNELS, n, PATCH, n, PATCH).transpose(0, 2, 4, 6, 1, 3, 5)
    x = x.reshape(TILES, KX, 128, PER_TILE * PATCHES).transpose(0, 2, 1, 3)
    xt = np.zeros((TILES, 128, KX, ROWS), f)
    xt[..., :PER_TILE * PATCHES] = x

    def chunks(w):
        return w.reshape(-1, 128, w.shape[1]).transpose(1, 0, 2).reshape(128, -1)

    def by_halves(w):
        return w.reshape(KD, 128, 2, 512).transpose(1, 2, 0, 3).reshape(128, -1)

    def padded(w, rows):
        return np.concatenate([w, np.zeros((rows - w.shape[0],) + w.shape[1:], w.dtype)])

    trees = "qkv"
    node_w = np.concatenate([padded(i[f"L0_ffn_{t}_node_w"], LEAVES) for t in trees])
    mats = {WT: chunks(i["L0_tok_W"].T), NODE_W: chunks(padded(node_w, 128).T)}
    attn = {WQ: by_halves(i["L0_attn_Wq"]), WK: by_halves(i["L0_attn_Wk"]), WV: by_halves(i["L0_attn_Wv"]),
            WO: chunks(i["L0_attn_Wo"])}
    ffn = {}
    for t, c in enumerate(trees):
        ffn[W1[t]] = by_halves(i[f"L0_ffn_{c}_w1"].transpose(1, 0, 2).reshape(D, HID))
        ffn[W2[t]] = chunks(i[f"L0_ffn_{c}_w2"].reshape(HID, D))
    weights = np.concatenate([(mats | (attn if n < P1_PIECES else ffn))[dst][:, off:off + width]
                              for n, (_, width, dst, _, off) in enumerate(PIECES)], 1)

    patch_rows, real = PER_TILE * PATCHES, PER_TILE * (PATCHES + 1)
    p = i["L0_tok_pos_embedding"][0]
    pos = np.zeros((2, ROWS, D), f)
    pos[0, :patch_rows] = np.tile(p[1:], (PER_TILE, 1))
    pos[0, patch_rows:real] = p[0]
    pos[1, :patch_rows] = i["L0_tok_b"]
    pos[1, patch_rows:real] = i["L0_tok_cls_token"][0, 0]
    image = np.concatenate([np.arange(patch_rows) // PATCHES, np.arange(ROWS - patch_rows)])
    same = image[:, None] == image[None, :]

    node_b = np.full((128,), -1.0, f)
    for t, c in enumerate(trees):
        node_b[LEAVES * t:LEAVES * t + NODES] = i[f"L0_ffn_{c}_node_b"]
    steer = np.zeros((128, 2, 128), f)
    thr = np.ones((2, 128), f)
    thr[0, ONE_ROW:ONE_ROW + 3] = 0.0
    e_mask = np.zeros((128, TREES, LEAVES, LEAF_W), f)
    for t in range(TREES):
        for leaf in range(LEAVES):
            off, sel = OFF_ROW + LEAVES * t + leaf, [row + LEAVES * t + leaf for row in SEL_ROWS]
            node, rights = leaf + NODES, 0
            while node:
                parent = (node - 1) // 2
                right = node == 2 * parent + 2
                rights += right
                steer[LEAVES * t + parent, 1, sel] = 1.0 if right else -1.0
                node = parent
            steer[:, 0, off] = -steer[:, 1, sel[0]]
            thr[1, sel], thr[0, off] = rights, 1 - rights
            e_mask[off, t, leaf] = -BIG
    cols = np.stack([*i["L0_attn_bq"].reshape(PAIRS, 128), *i["L0_attn_bk"].reshape(PAIRS, 128), node_b, *thr], 1)
    b2 = np.zeros((128, TREES, D), f)
    for t, c in enumerate(trees):
        for row in SEL_ROWS:
            b2[row + LEAVES * t:row + LEAVES * (t + 1), t] = i[f"L0_ffn_{c}_b2"]
    bf = mybir.dt.np(mybir.dt.bfloat16)
    return dict(
        x=xt.reshape(TILES, 128, -1), weights=weights, pos=pos[0], tok=pos[1], ident=np.eye(128, dtype=f),
        mask=np.where(same, f(HD ** -0.5), f(0)), mask_bias=np.where(same, f(0), f(-1e30)),
        bv=np.tile(i["L0_attn_bv"], (ROWS, 1)), bo=np.tile(i["L0_attn_bo"], (ROWS, 1)), cols=cols.astype(f),
        e_mask=e_mask.reshape(128, -1).astype(bf), b1=np.stack([i[f"L0_ffn_{c}_b1"].reshape(-1) for c in trees]),
        b2=b2.reshape(128, -1), steer=steer.reshape(128, -1).astype(bf))


def kernel(**inputs):
    import concourse.bacc as bacc
    from concourse.bass_utils import run_bass_kernel_spmd

    arrays = {k: np.ascontiguousarray(v) for k, v in launch_arrays({k: np.asarray(v) for k, v in inputs.items()}).items()}
    nc = bacc.Bacc("TRN2", target_bir_lowering=False, num_devices=1)
    args = {k: nc.dram_tensor(k, a.shape, mybir.dt.from_np(a.dtype), kind="ExternalInput").ap() for k, a in arrays.items()}
    out = nc.dram_tensor("out", (TILES, ROWS, D), mybir.dt.float32, kind="ExternalOutput").ap()
    build_program(nc, *args.values(), out)
    got = run_bass_kernel_spmd(nc, [arrays], core_ids=[0]).results[0]["out"]
    patch_rows, real = PER_TILE * PATCHES, PER_TILE * (PATCHES + 1)
    patches = got[:, :patch_rows].reshape(TILES * PER_TILE, PATCHES, D)
    return np.concatenate([got[:, patch_rows:real].reshape(TILES * PER_TILE, 1, D), patches], 1)[:IMAGES]
```

```python
import concourse.bass as bass
from concourse import mybir
from contextlib import ExitStack
import numpy as np

IMAGES, CHANNELS, SIDE, PATCH, D = 64, 3, 96, 16, 256
PATCHES = (SIDE // PATCH) ** 2
PER_TILE = 3
ROWS = PER_TILE * (PATCHES + 1) + 1
TILES = -(-IMAGES // PER_TILE)
GT = 4
GROUPS = -(-TILES // GT)
TAIL = TILES - GT * (GROUPS - 1)
W = GT * ROWS
KX = CHANNELS * PATCH * PATCH // 128
KD = D // 128
HEADS, HD = 16, 64
PAIRS = HEADS // 2
INNER = HEADS * HD
TREES, LEAVES, NODES, LEAF_W, DEPTH = 3, 16, 15, 64, 4
HID = LEAVES * LEAF_W
CH = HID // 128
BIG = 2.0 ** 126
QUAD = 4
QUADS = TREES * CH // QUAD - 1
PLACES = 3
EPS = 1e-5

OFF_ROW = 0
ONE_ROW = 48
SEL_ROWS = (0, 64)

XHI, XLO = 0, GT * KX * ROWS
WT = 2 * GT * KX * ROWS
WQ = WT + 2 * KX * D
WSIZE = 2 * KD * INNER
WK, WV, WO = WQ + WSIZE, WQ + 2 * WSIZE, WQ + 3 * WSIZE
ARENA = WO + WSIZE
W1 = [0, WQ, WV]
W2 = [WSIZE, WK, WO]

STAGE = 1024
NODE_W = -1
PIECES, _at = [], 0
_HALVES = [(w, WSIZE // 2, half * STAGE, STAGE) for half in range(2) for w in (WV, WQ, WK, WO)]
_TREES = [(w, WSIZE // 2, half * STAGE, STAGE) for t in range(TREES) for w in (W1[t], W2[t]) for half in range(2)]
for _dst, _size, _off, _n in [(WT, KX * D, 0, STAGE), (WT, KX * D, STAGE, KX * D - STAGE), *_HALVES,
                              (NODE_W, KD * 128, 0, KD * 128), *_TREES]:
    PIECES.append((_at, _n, _dst, _size, _off))
    _at += _n
WT_PIECES = 2
HALF_PIECES = 4
P1_PIECES = WT_PIECES + 2 * HALF_PIECES + 1
SLOTS = 4
EARLY = P1_PIECES + 4


CONSTS = 4
CONSTS2 = 5


def first_group(g):
    return isinstance(g, int) and g == 0


def before_tail(g):
    return isinstance(g, int) and g == GROUPS - 2


def build_program(nc, x, weights, pos, tok, ident, mask, mask_bias, bv, bo, cols, e_mask, b1, b2, steer, out):
    f32, f32r, bf16 = mybir.dt.float32, mybir.dt.float32r, mybir.dt.bfloat16
    ALU, ACT, AX = mybir.AluOpType, mybir.ActivationFunctionType, mybir.AxisListType
    R = ROWS
    HW = GT * R // 2

    with ExitStack() as ctx:
        def sb(name, shape, dt=f32):
            return ctx.enter_context(nc.sbuf_tensor("sb_" + name, shape, dt))

        def sem(name):
            return ctx.enter_context(nc.semaphore(name))

        arena = sb("arena", [128, ARENA], f32r)
        node_w = sb("node_w", [128, 2, KD, 128], f32r)
        xT = sb("xT", [128, 2, KD, W], f32r)
        pairT = sb("pairT", [128, 3, 2, W], f32r)
        e_sb = sb("e_sb", [128, QUAD * 128], bf16)
        mask_own = sb("mask_own", [128, QUAD * W], bf16)
        b2_sb = sb("b2_sb", [128, TREES, D], f32r)
        routeT = sb("routeT", [128, W], bf16)
        selT = sb("selT", [128, W], f32r)
        bitsT = sb("bitsT", [128, W], bf16)
        steer_sb = sb("steer_sb", [128, 256], bf16)
        x_raw = sb("x_raw", [128, GT, KX * R])
        x_flat = x_raw[:, :, :].rearrange("p t n -> p (t n)")
        h_all = sb("h_all", [128, TILES, D])
        xn = sb("xn", [R, GT, D])
        q_pad = sb("q_pad", [128, 2, 2, GT, 2, R], f32r)
        k_high = sb("k_high", [128, 2, W], f32r)
        v_sb = sb("v_sb", [128, 2, GT, D])
        s_sb = sb("s_sb", [128, 2, GT, 2 * R])
        bv_sb = sb("bv_sb", [128, INNER])
        bo_sb = sb("bo_sb", [R, D])
        pos_sb = sb("pos_sb", [R, D])
        mask_sb = sb("mask_sb", [R, R])
        maskb_sb = sb("maskb_sb", [R, R])
        id_sb = sb("id_sb", [128, 128])
        cols_sb = sb("cols_sb", [128, 2 * PAIRS + 4 + TREES * CH])
        stats = sb("stats", [R, GT, 6])
        mv = sb("mv", [R, GT, 2])
        bearer = sb("bearer", [R, 3])
        std = sb("std", [R, GT])
        rstd = sb("rstd", [R, GT])
        mean2 = sb("mean2", [R, TILES])
        var2 = sb("var2", [R, TILES])
        std2 = sb("std2", [R, TILES])
        rstd2 = sb("rstd2", [R, TILES])
        neg_max = sb("neg_max", [R, GT])
        row_sum = sb("row_sum", [R, GT])
        row_inv = sb("row_inv", [R, GT])
        h_stage = h_all[:, 3 * GT:5 * GT, :].rearrange("p t n -> p (t n)")
        k_low = pairT[:, 2, :, :]
        first_stage = h_all[:, GT:5 * GT, :].rearrange("p t n -> p (t n)")
        v_stage = v_sb[:, :, :, :].rearrange("p a t n -> p a (t n)")
        s_stage = s_sb[:, :, :, :].rearrange("p a t n -> p (a t n)")
        qT = x_flat[:, 0:2 * KD * W].rearrange("p (z k w) -> p z k w", z=2, k=KD)
        soft_in = s_sb[0:R, 0, 0:2, :].rearrange("p a b -> p (a b)")
        probs = s_sb[0:R, 0, 2:4, :].rearrange("p a b -> p (a b)")
        probsT = s_sb[0:R, 1, 0:2, :].rearrange("p a b -> p (a b)")
        v2 = v_sb[0:R, 0, :, :]
        out_sb = v_sb[0:R, 1, :, :]

        masks = [m.rearrange("p (c w) -> p c w", c=QUAD) for m in
                 (mask_own[:, :], bv_sb[:, 0:QUAD * W // 2].bitcast(bf16),
                  x_flat[:, 2 * KD * W:2 * KD * W + QUAD * W // 2].bitcast(bf16))]

        banks = [ctx.enter_context(nc.psum_tensor(f"bank{i}", [128, 512], f32)) for i in range(8)]
        ring = banks[0:2]
        wo_acc = banks[2:4]
        s_ps = banks[4:6]
        o_ps = banks[6:8]
        hid_ps = [banks[4], banks[3], banks[2]]
        down = banks[5:7]
        side = banks[7]

        consts = sem("consts")
        consts2 = sem("consts2")
        pos_ready = sem("pos_ready")
        bias_in = sem("bias_in")
        bias_step = sem("bias_step")
        bias_rows = sem("bias_rows")
        prelude = sem("prelude")
        x_loaded = [sem("x_loaded0"), sem("x_loaded1")]
        staged = [sem(f"staged{i}") for i in range(SLOTS)]
        staged2 = [sem(f"staged2_{i}") for i in range(2)]
        staged3 = [sem(f"staged3_{i}") for i in range(2)]
        piece_hi = sem("piece_hi")
        piece_lo = sem("piece_lo")
        x_hi = sem("x_hi")
        x_lo = sem("x_lo")
        tok_done = sem("tok_done")
        h_ready = sem("h_ready")
        stat_step = sem("stat_step")
        var_ready = sem("var_ready")
        std_ready = sem("std_ready")
        xn_ready = sem("xn_ready")
        bo_added = sem("bo_added")
        centred = sem("centred")
        t_done = sem("t_done")
        xT_hi = sem("xT_hi")
        xT_lo = sem("xT_lo")
        v_done = sem("v_done")
        v_ready = sem("v_ready")
        q_done = sem("q_done")
        q_hi = sem("q_hi")
        k_hi = sem("k_hi")
        q_ready = sem("q_ready")
        k_done = sem("k_done")
        k_ready = sem("k_ready")
        s_done = sem("s_done")
        s_ready = sem("s_ready")
        o_done = sem("o_done")
        o_hi = sem("o_hi")
        o_lo = sem("o_lo")
        wo_done = sem("wo_done")
        h2_ready = sem("h2_ready")
        var2_ready = sem("var2_ready")
        std2_ready = sem("std2_ready")
        rstd2_ready = sem("rstd2_ready")
        score_done = sem("score_done")
        bits_ready = sem("bits_ready")
        count_done = sem("count_done")
        route_ready = sem("route_ready")
        up_done = sem("up_done")
        spread = [sem(f"spread{i}") for i in range(PLACES)]
        masked = sem("masked")
        hid_hi = sem("hid_hi")
        hid_lo = sem("hid_lo")
        down_done = sem("down_done")
        down_q = sem("down_q")
        down_v = sem("down_v")
        att_done = sem("att_done")
        soft_step = sem("soft_step")
        max_ready = sem("max_ready")
        exp_ready = sem("exp_ready")
        pt_done = sem("pt_done")
        pt_ready = sem("pt_ready")
        av_done = sem("av_done")
        out_ready = sem("out_ready")
        stored = sem("stored")

        def part(base, size, low):
            return arena[:, base + low * size:base + (low + 1) * size]

        def tok_w(k, low):
            return part(WT, KX * D, low)[:, k * D:(k + 1) * D]

        def in_w(base, k, c, n, low):
            at = c // 512 * STAGE + k * 512 + c % 512
            return part(base, KD * INNER, low)[:, at:at + n]

        def out_w(base, c, m, n, low):
            return part(base, CH * D, low)[:, c * D + m:c * D + m + n]

        def piece_dst(i, low):
            _, n, dst, size, off = PIECES[i]
            if dst == NODE_W:
                return node_w[:, low, :, :].rearrange("p k n -> p (k n)")
            return part(dst, size, low)[:, off:off + n]

        def slot(i):
            n = PIECES[i][1]
            if i < P1_PIECES:
                at, arrived, turn = i % SLOTS, staged, i // SLOTS + 1
                dst = first_stage[:, at * STAGE:at * STAGE + n]
            elif i < EARLY:
                at, arrived, turn = (i - P1_PIECES) % 2, staged2, (i - P1_PIECES) // 2 + 1
                dst = x_flat[:, at * STAGE:at * STAGE + n]
            else:
                at, arrived, turn = (i - EARLY) % 2, staged3, (i - EARLY) // 2 + 1
                dst = (v_stage[:, 1, 0:n], s_stage[:, 0:n])[at]
            return dst, arrived[at], 16 * turn

        PRODUCTS = [(0, 0), (0, 1), (1, 0)]

        def tiles_of(g, lo, n):
            return bass.ds(g * GT + lo, n)

        def embed_bank(nt, tp):
            return ring[tp if nt == GT else 1]

        def v_bank(nt, quarter, tp):
            if nt == GT:
                return ring[tp]
            return wo_acc[1] if quarter >= 2 else ring[1 - quarter]

        def qk_banks(nt, j):
            if j == 0:
                return s_ps[0], s_ps[1]
            return (o_ps[1], s_ps[1]) if nt < GT and j % 2 == 0 else (ring[0], ring[1])

        def late_pieces(g, j):
            i = P1_PIECES - 4 + j - 2
            return (i,) if first_group(g) and 2 <= j <= 5 else ()

        def for_groups(eng, body):
            body(0, GT, GT)
            with eng.Fori(1, GROUPS - 2) as g:
                body(g, GT, GT)
            body(GROUPS - 2, GT, TAIL)
            body(GROUPS - 1, TAIL, 0)

        block = ctx.enter_context(nc.Block())

        @block.sync
        def _(sp):
            def load_x(g, half):
                sp.dma_start(x_raw[:, 2 * half:2 * half + 2, :],
                             x[tiles_of(g, 2 * half, 2), :, :].rearrange("t p n -> p t n")).then_inc(x_loaded[half], 16)

            def load_piece(i):
                at, n, _, _, _ = PIECES[i]
                dst, arrived, _ = slot(i)
                if SLOTS <= i < P1_PIECES:
                    sp.wait_ge(piece_lo, i + 1 - SLOTS)
                if P1_PIECES + 2 <= i < EARLY or i >= EARLY + 2:
                    sp.wait_ge(piece_lo, i - 1)
                sp.dma_start(dst, weights[:, at:at + n]).then_inc(arrived, 16)

            load_x(0, 0)
            load_piece(0)
            load_piece(1)
            load_x(0, 1)
            for i in range(WT_PIECES, SLOTS):
                load_piece(i)
            for dst, src in ((pos_sb, pos), (xn[:, 0, :], tok), (id_sb, ident), (cols_sb, cols)):
                sp.dma_start(dst[:, :], src[:, :]).then_inc(consts, 16)
            for i in range(SLOTS, P1_PIECES):
                if i == 2 * SLOTS:
                    sp.wait_ge(x_lo, 2)
                    load_x(1, 0)
                    load_x(1, 1)
                load_piece(i)
                if i == SLOTS:
                    for dst, src in ((bo_sb, bo), (bv_sb, bv), (mask_sb, mask), (maskb_sb, mask_bias), (steer_sb, steer)):
                        sp.dma_start(dst[0:src.shape[0], :], src[:, :]).then_inc(consts2, 16)

            with sp.Fori(2, GROUPS - 1) as g:
                sp.wait_ge(x_lo, 2 * g)
                load_x(g, 0)
                load_x(g, 1)
            sp.wait_ge(x_lo, 2 * (GROUPS - 1))
            load_x(GROUPS - 1, 0)
            sp.wait_ge(x_lo, 2 * (GROUPS - 1) + 1)
            for i in range(P1_PIECES, EARLY):
                load_piece(i)
            sp.wait_ge(o_done, PAIRS * (2 * (GROUPS - 1) + TAIL // 2))
            for i in range(EARLY, EARLY + 2):
                load_piece(i)

            def spread_masks(g, nt, q):
                for c in range(QUAD):
                    row = OFF_ROW + 2 * (QUAD * (q + 1) + c)
                    sp.dma_start(masks[q % PLACES][:, c, 0:nt * R],
                                 routeT[row:row + 2, 0:nt * R].unsqueeze(1).to_broadcast([2, LEAF_W, nt * R])
                                 ).then_inc(spread[q % PLACES], 16)

            def store(g, nt):
                sp.wait_ge(out_ready, 2 * g + nt // 2)
                sp.dma_start(out[tiles_of(g, 0, nt), :, :].rearrange("t p n -> p t n"),
                             out_sb[:, 0:nt, :]).then_inc(stored, 16)

            def early_masks(g, nt):
                sp.wait_ge(route_ready, 2 * g + 1)
                for q in range(PLACES):
                    if first_group(g) and q == 2:
                        sp.wait_ge(piece_lo, EARLY)
                    spread_masks(g, nt, q)

            def late_masks(g, nt):
                for q in range(PLACES, QUADS):
                    sp.wait_ge(masked, QUADS * QUAD * g + QUAD * (q - PLACES + 1))
                    spread_masks(g, nt, q)

            early_masks(0, GT)
            for i in range(EARLY + 2, len(PIECES)):
                load_piece(i)
            late_masks(0, GT)
            with sp.Fori(1, GROUPS - 1) as g:
                early_masks(g, GT)
                store(g - 1, GT)
                late_masks(g, GT)
            early_masks(GROUPS - 1, TAIL)
            store(GROUPS - 2, GT)
            late_masks(GROUPS - 1, TAIL)
            store(GROUPS - 1, TAIL)
            sp.wait_ge(stored, 16 * GROUPS)

        @block.gpsimd
        def _(pool):
            nc.gpsimd.memset(q_pad[:, :, :, :, :, :].bitcast(f32), 0.0).then_inc(prelude, 1)

            def split_biases():
                n = QUAD * 128
                b1_raw = h_stage[0:1, 0:n]
                b2_raw = h_stage[:, STAGE:STAGE + TREES * D]
                b1_parts = [h_stage[0:1, STAGE + i * n // 2:STAGE + (i + 1) * n // 2].bitcast(bf16) for i in range(2)]
                pool.wait_ge(piece_lo, P1_PIECES)
                pool.dma_start(b1_raw, b1[:, :]).then_inc(bias_in, 16)
                pool.dma_start(b2_raw, b2[:, :]).then_inc(bias_in, 16)
                pool.dma_start(e_sb[:, :], e_mask[:, :]).then_inc(bias_in, 16)
                pool.wait_ge(bias_in, 48)
                b2_all = b2_sb[:, :, :].rearrange("p t n -> p (t n)")
                low = slice(SEL_ROWS[1], 128)
                nc.gpsimd.tensor_copy(b2_all, b2_raw).then_inc(bias_step, 1)
                pool.wait_ge(bias_step, 1)
                nc.gpsimd.tensor_tensor(b2_all[low, :], b2_raw[low, :], b2_all[low, :].bitcast(f32),
                                        ALU.subtract).then_inc(bias_step, 1)
                pool.wait_ge(bias_step, 2)
                for i in range(3):
                    piece = b1_parts[i % 2]
                    if i == 2:
                        pool.wait_ge(bias_rows, 32)
                    nc.gpsimd.tensor_copy(piece, b1_raw).then_inc(bias_step, 1)
                    pool.wait_ge(bias_step, 2 * i + 3)
                    pool.dma_start(e_sb[ONE_ROW + i:ONE_ROW + i + 1, :], piece).then_inc(bias_rows, 16)
                    if i < 2:
                        nc.gpsimd.tensor_tensor(b1_raw, b1_raw, piece, ALU.subtract).then_inc(bias_step, 1)
                        pool.wait_ge(bias_step, 2 * i + 4)

            pool.wait_ge(consts2, 16 * CONSTS2)

            def add_bo(g, nt):
                pool.wait_ge(xn_ready, g + 1)
                h = h_all[0:R, tiles_of(g, 0, nt), :]
                nc.gpsimd.tensor_tensor(h, h, bo_sb[:, :].unsqueeze(1).to_broadcast([R, nt, D]), ALU.add).then_inc(bo_added, 1)

            def x_split_lo(g, half):
                pool.wait_ge(x_hi, 2 * g + half + 1)
                n = 2 * KX * R
                nc.gpsimd.tensor_tensor(arena[:, XLO + half * n:XLO + (half + 1) * n],
                                        x_raw[:, 2 * half:2 * half + 2, :].rearrange("p t n -> p (t n)"),
                                        arena[:, XHI + half * n:XHI + (half + 1) * n].bitcast(f32),
                                        ALU.subtract).then_inc(x_lo, 1)

            add_bo(0, GT)
            x_split_lo(1, 0)
            x_split_lo(1, 1)
            split_biases()
            add_bo(1, GT)
            with pool.Fori(2, GROUPS - 1) as g:
                x_split_lo(g, 0)
                x_split_lo(g, 1)
                add_bo(g, GT)
            x_split_lo(GROUPS - 1, 0)
            add_bo(GROUPS - 1, TAIL)

            def split_piece(i):
                src, arrived, value = slot(i)
                pool.wait_ge(arrived, value)
                nc.gpsimd.tensor_copy(piece_dst(i, 0), src).then_inc(piece_hi, 1)
                pool.wait_ge(piece_hi, i + 1)
                nc.gpsimd.tensor_tensor(piece_dst(i, 1), src, piece_dst(i, 0).bitcast(f32), ALU.subtract).then_inc(piece_lo, 1)

            def split_piece_lo(i):
                src, _, _ = slot(i)
                pool.wait_ge(piece_hi, i + 1)
                nc.gpsimd.tensor_tensor(piece_dst(i, 1), src, piece_dst(i, 0).bitcast(f32), ALU.subtract).then_inc(piece_lo, 1)

            def normalise(g, nt):
                pool.wait_ge(rstd2_ready, g + 1)
                pool.wait_ge(t_done, KD * (GROUPS + g))
                cut = tiles_of(g, 0, nt)
                nc.gpsimd.tensor_tensor(xn[:, 0:nt, :], h_all[0:R, cut, :], mean2[:, cut].unsqueeze(2).to_broadcast([R, nt, D]),
                                        ALU.subtract).then_inc(centred, 1)
                pool.wait_ge(centred, g + 1)
                nc.gpsimd.tensor_tensor(xn[:, 0:nt, :], xn[:, 0:nt, :], rstd2[:, cut].unsqueeze(2).to_broadcast([R, nt, D]),
                                        ALU.mult).then_inc(xn_ready, 1)

            normalise(0, GT)
            pool.wait_ge(tok_done, 2 * (GROUPS - 1) + TAIL // 2)
            for i in range(P1_PIECES, EARLY):
                split_piece(i)
            for i in range(EARLY, len(PIECES)):
                split_piece_lo(i)
            with pool.Fori(1, GROUPS - 1) as g:
                normalise(g, GT)
            normalise(GROUPS - 1, TAIL)

        @block.scalar
        def _(act):
            def split_hi(i):
                src, arrived, value = slot(i)
                act.wait_ge(arrived, value)
                nc.scalar.activation(piece_dst(i, 0), src, ACT.Copy).then_inc(piece_hi, 1)

            def x_split_hi(g, half):
                act.wait_ge(x_loaded[half], 16 * (g + 1))
                if not first_group(g):
                    act.wait_ge(tok_done, 2 * g)
                n = 2 * KX * R
                nc.scalar.activation(arena[:, XHI + half * n:XHI + (half + 1) * n],
                                     x_raw[:, 2 * half:2 * half + 2, :].rearrange("p t n -> p (t n)"),
                                     ACT.Copy).then_inc(x_hi, 1)

            def root(g, nt):
                act.wait_ge(var_ready, g + 1)
                nc.scalar.activation(std[:, 0:nt], mv[:, 0:nt, 1], ACT.Sqrt).then_inc(std_ready, 1)

            def transposed_hi(n, nt):
                for k in range(KD):
                    act.wait_ge(t_done, KD * n + k + 1)
                    nc.scalar.activation(xT[:, 0, k, 0:nt * R], ring[k][:, 0:nt * R], ACT.Copy).then_inc(xT_hi, 1)

            def q_evac_hi(g, nt, j):
                act.wait_ge(q_done, PAIRS * g + j + 1)
                if j >= 2:
                    act.wait_ge(s_done, 2 * PAIRS * g + nt // 2 * (j - 1))
                for half in range(2):
                    rows = slice(HD * half, HD * (half + 1))
                    last = nc.scalar.activation(q_pad[rows, 0, j % 2, 0:nt, half, :],
                                                qk_banks(nt, j)[0][rows, 0:nt * R].rearrange("p (t r) -> p t r", r=R),
                                                ACT.Identity, bias=cols_sb[rows, j:j + 1])
                last.then_inc(q_hi, 1)

            def k_evac_hi(g, nt, j):
                act.wait_ge(k_done, PAIRS * g + j + 1)
                nc.scalar.activation(k_high[:, j % 2, 0:nt * R], qk_banks(nt, j)[1][:, 0:nt * R], ACT.Identity,
                                     bias=cols_sb[:, PAIRS + j:PAIRS + j + 1]).then_inc(k_hi, 1)

            def o_evac_hi(g, nt, j):
                if j >= 2:
                    act.wait_ge(wo_done, PAIRS * g + j - 1)
                for tp in range(nt // 2):
                    act.wait_ge(o_done, 2 * PAIRS * g + nt // 2 * j + tp + 1)
                    for half in range(2):
                        rows = slice(HD * half, HD * (half + 1))
                        src = o_ps[tp][rows, 0:2 * HW].rearrange("p (t h r) -> p t h r", t=2, h=2)
                        last = nc.scalar.activation(
                            pairT[rows, j % 2, 0, tp * HW:(tp + 1) * HW].rearrange("p (t r) -> p t r", r=R),
                            src[:, :, half, :], ACT.Copy)
                    last.then_inc(o_hi, 1)

            x_split_hi(0, 0)
            split_hi(0)
            split_hi(1)
            x_split_hi(0, 1)
            for i in range(2, 6):
                split_hi(i)
            root(0, GT)
            transposed_hi(0, GT)
            split_hi(6)
            q_evac_hi(0, GT, 0)
            k_evac_hi(0, GT, 0)

            def attention(g, nt, nxt):
                for j in range(1, PAIRS + 2):
                    if j < PAIRS:
                        q_evac_hi(g, nt, j)
                        k_evac_hi(g, nt, j)
                    for i in late_pieces(g, j):
                        split_hi(i)
                    if j in (1, 2) and 2 * (j - 1) < nxt:
                        x_split_hi(g + 1, j - 1)
                    if j == 8:
                        transposed_hi(g + 1, nxt or GT)
                    if j >= 2:
                        o_evac_hi(g, nt, j - 2)
                    if j == (5 if nt == GT else 9) and not first_group(g):
                        root2(g - 1, GT)
                    if j == 6 and nxt:
                        root(g + 1, nxt)
                    if j == PAIRS + 1 and nxt:
                        q_evac_hi(g + 1, nxt, 0)
                        k_evac_hi(g + 1, nxt, 0)

            def root2(g, nt):
                act.wait_ge(var2_ready, g + 1)
                nc.scalar.activation(std2[:, tiles_of(g, 0, nt)], var2[:, tiles_of(g, 0, nt)], ACT.Sqrt).then_inc(std2_ready, 1)

            for_groups(act, attention)
            root2(GROUPS - 1, TAIL)

            def hidden_hi(g, nt, s):
                if s < QUAD:
                    act.wait_ge(up_done, 3 * CH * g + s + 1)
                else:
                    act.wait_ge(masked, QUADS * QUAD * g + s - QUAD + 1)
                if s >= 3:
                    act.wait_ge(down_done, 3 * CH * g + s - 2)
                nc.scalar.activation(pairT[:, s % 3, 0, 0:nt * R], hid_ps[s % 3][:, 0:nt * R], ACT.Relu).then_inc(hid_hi, 1)

            def probs_out(g, nt):
                act.wait_ge(pt_done, g + 1)
                nc.scalar.activation(probsT[:, 0:nt * R], ring[1][0:R, 0:nt * R], ACT.Copy).then_inc(pt_ready, 1)

            def ffn(g, nt, nxt, first=False):
                for s in range(TREES * CH + 2):
                    if s < TREES * CH:
                        hidden_hi(g, nt, s)
                    if first and s % 2 == 0 and EARLY + s // 2 < len(PIECES):
                        if s == 0:
                            act.wait_ge(piece_lo, EARLY)
                            act.wait_ge(q_done, PAIRS * GROUPS)
                            act.wait_ge(k_done, PAIRS * GROUPS)
                            act.wait_ge(wo_done, PAIRS * GROUPS)
                        split_hi(EARLY + s // 2)
                    for tree in range(2):
                        if s == CH * (tree + 1) + 1:
                            act.wait_ge(down_done, 3 * CH * g + CH * (tree + 1))
                            for m in range(KD):
                                last = nc.scalar.activation(qT[:, tree, m, 0:nt * R], down[m][:, 0:nt * R], ACT.Copy)
                            last.then_inc(down_q, 1)
                    if s == 2 and not first:
                        exps(g - 1, GT)
                    if s == 5 and not first:
                        probs_out(g - 1, GT)
                    if not nxt and s == 2 * CH + 5:
                        exps(g, nt)
                    if not nxt and s == TREES * CH + 1:
                        probs_out(g, nt)
                    if s == TREES * CH and nxt:
                        transposed_hi(GROUPS + g + 1, nxt)

            def exps(g, nt):
                act.wait_ge(max_ready, g + 1)
                for t in range(nt):
                    last = nc.scalar.activation(probs[:, t * R:(t + 1) * R], soft_in[:, t * R:(t + 1) * R], ACT.Exp,
                                                bias=neg_max[:, t:t + 1], accum_out=row_sum[:, t:t + 1])
                last.then_inc(exp_ready, 1)

            ffn(0, GT, GT, first=True)
            with act.Fori(1, GROUPS - 2) as g:
                ffn(g, GT, GT)
            ffn(GROUPS - 2, GT, TAIL)
            ffn(GROUPS - 1, TAIL, 0)

        @block.vector
        def _(dve):
            def split_lo(i):
                src, _, _ = slot(i)
                dve.wait_ge(piece_hi, i + 1)
                nc.vector.tensor_tensor(piece_dst(i, 1), src, piece_dst(i, 0).bitcast(f32),
                                        ALU.subtract).then_inc(piece_lo, 1)

            def x_split_lo(g, half):
                dve.wait_ge(x_hi, 2 * g + half + 1)
                n = 2 * KX * R
                nc.vector.tensor_tensor(arena[:, XLO + half * n:XLO + (half + 1) * n],
                                        x_raw[:, 2 * half:2 * half + 2, :].rearrange("p t n -> p (t n)"),
                                        arena[:, XHI + half * n:XHI + (half + 1) * n].bitcast(f32),
                                        ALU.subtract).then_inc(x_lo, 1)

            def embed(g, nt, tp):
                dve.wait_ge(tok_done, 2 * g + tp + 1)
                nc.vector.tensor_tensor(h_all[0:R, tiles_of(g, 2 * tp, 2), :],
                                        embed_bank(nt, tp)[0:R, :].rearrange("p (t n) -> p t n", t=2),
                                        pos_sb[:, :].unsqueeze(1).to_broadcast([R, 2, D]), ALU.add).then_inc(h_ready, 1)

            def half_moments(g, tp):
                dve.wait_ge(h_ready, 2 * g + tp + 1)
                nc.vector.memset(bearer[:, tp:tp + 1], 0.0)
                for t in (2 * tp, 2 * tp + 1):
                    last = nc.vector.bn_stats(stats[:, t, :], h_all[0:R, tiles_of(g, t, 1), :].rearrange("p t n -> p (t n)"))
                last.then_inc(stat_step, 1)

            def moments(g, nt):
                base = 2 if first_group(g) else 6 * g - 2 + nt // 2
                if not first_group(g):
                    for tp in range(nt // 2):
                        half_moments(g, tp)
                dve.wait_ge(stat_step, base)
                nc.vector.memset(bearer[:, 2:3], 0.0)
                for t in range(nt):
                    last = nc.vector.bn_aggr(mv[:, t, :], stats[:, t, :])
                last.then_inc(stat_step, 1)
                dve.wait_ge(stat_step, base + 1)
                nc.vector.tensor_scalar(mv[:, 0:nt, 1], mv[:, 0:nt, 1], EPS, None, ALU.add).then_inc(var_ready, 1)

            def normalise(g, nt):
                dve.wait_ge(std_ready, g + 1)
                nc.vector.reciprocal(rstd[:, 0:nt], std[:, 0:nt]).then_inc(stat_step, 1)
                dve.wait_ge(stat_step, 4 if first_group(g) else 6 * g + nt // 2)
                if not first_group(g):
                    dve.wait_ge(t_done, KD * g)
                for t in range(nt):
                    last = nc.vector.tensor_scalar(xn[:, t, :], h_all[0:R, tiles_of(g, t, 1), :].rearrange("p t n -> p (t n)"),
                                                   mv[:, t, 0:1], rstd[:, t:t + 1], ALU.subtract, ALU.mult)
                last.then_inc(xn_ready, 1)

            def transposed_lo(n, nt):
                for k in range(KD):
                    dve.wait_ge(xT_hi, KD * n + k + 1)
                    nc.vector.tensor_tensor(xT[:, 1, k, 0:nt * R], ring[k][:, 0:nt * R],
                                            xT[:, 0, k, 0:nt * R].bitcast(f32), ALU.subtract).then_inc(xT_lo, 1)

            def v_evac(g, nt, quarter, tp):
                if quarter >= 2:
                    dve.wait_ge(o_done, 2 * PAIRS * g + nt // 2 * (2 * quarter - 2))
                dve.wait_ge(v_done, PAIRS * g + nt // 2 * quarter + tp + 1)
                nc.vector.tensor_tensor(v_sb[0:R, quarter % 2, 2 * tp:2 * tp + 2, :],
                                        v_bank(nt, quarter, tp)[0:R, :].rearrange("p (t n) -> p t n", t=2),
                                        bv_sb[0:R, quarter * D:(quarter + 1) * D].unsqueeze(1).to_broadcast([R, 2, D]),
                                        ALU.add).then_inc(v_ready, 1)

            def q_evac_lo(g, nt, j):
                dve.wait_ge(q_hi, PAIRS * g + j + 1)
                for half in range(2):
                    rows = slice(HD * half, HD * (half + 1))
                    last = nc.vector.scalar_tensor_tensor(q_pad[rows, 1, j % 2, 0:nt, half, :],
                                                          qk_banks(nt, j)[0][rows, 0:nt * R].rearrange("p (t r) -> p t r", r=R),
                                                          cols_sb[rows, j:j + 1],
                                                          q_pad[rows, 0, j % 2, 0:nt, half, :].bitcast(f32),
                                                          ALU.add, ALU.subtract)
                last.then_inc(q_ready, 1)

            def k_evac_lo(g, nt, j):
                dve.wait_ge(k_hi, PAIRS * g + j + 1)
                nc.vector.scalar_tensor_tensor(k_low[:, j % 2, 0:nt * R], qk_banks(nt, j)[1][:, 0:nt * R],
                                               cols_sb[:, PAIRS + j:PAIRS + j + 1], k_high[:, j % 2, 0:nt * R].bitcast(f32),
                                               ALU.add, ALU.subtract).then_inc(k_ready, 1)

            def s_evac(g, nt, j):
                if j >= 2:
                    dve.wait_ge(o_done, 2 * PAIRS * g + nt // 2 * (j - 1))
                for tp in range(nt // 2):
                    dve.wait_ge(s_done, 2 * PAIRS * g + nt // 2 * j + tp + 1)
                    nc.vector.tensor_tensor(s_sb[0:R, j % 2, 2 * tp:2 * tp + 2, :].rearrange("p t (h r) -> p (t h) r", h=2),
                                            s_ps[tp][0:R, 0:2 * HW].rearrange("p (b r) -> p b r", r=R),
                                            mask_sb[:, :].unsqueeze(1).to_broadcast([R, 4, R]), ALU.mult).then_inc(s_ready, 1)

            def o_evac_lo(g, nt, j):
                for tp in range(nt // 2):
                    dve.wait_ge(o_hi, 2 * PAIRS * g + nt // 2 * j + tp + 1)
                    for half in range(2):
                        rows = slice(HD * half, HD * (half + 1))
                        src = o_ps[tp][rows, 0:2 * HW].rearrange("p (t h r) -> p t h r", t=2, h=2)
                        cut = slice(tp * HW, (tp + 1) * HW)
                        last = nc.vector.tensor_tensor(
                            pairT[rows, j % 2, 1, cut].rearrange("p (t r) -> p t r", r=R), src[:, :, half, :],
                            pairT[rows, j % 2, 0, cut].bitcast(f32).rearrange("p (t r) -> p t r", r=R), ALU.subtract)
                    last.then_inc(o_lo, 1)

            def residual(g, nt):
                dve.wait_ge(wo_done, PAIRS * (g + 1))
                dve.wait_ge(bo_added, g + 1)
                for tp in range(nt // 2):
                    h = h_all[0:R, tiles_of(g, 2 * tp, 2), :]
                    nc.vector.tensor_tensor(h, wo_acc[tp][0:R, :].rearrange("p (t n) -> p t n", t=2), h, ALU.add).then_inc(h2_ready, 1)

            def moments2(g, nt):
                dve.wait_ge(h2_ready, 2 * g + nt // 2)
                nc.vector.memset(bearer[:, 0:1], 0.0)
                for t in range(nt):
                    last = nc.vector.bn_stats(stats[:, t, :], h_all[0:R, tiles_of(g, t, 1), :].rearrange("p t n -> p (t n)"))
                last.then_inc(stat_step, 1)
                base = 6 * g + (3 if nt < GT else 7 if before_tail(g) else 8)
                dve.wait_ge(stat_step, base + 1)
                nc.vector.memset(bearer[:, 1:2], 0.0)
                for t in range(nt):
                    last = nc.vector.bn_aggr(mv[:, t, :], stats[:, t, :])
                last.then_inc(stat_step, 1)
                dve.wait_ge(stat_step, base + 2)
                nc.vector.tensor_copy(mean2[:, tiles_of(g, 0, nt)], mv[:, 0:nt, 0])
                nc.vector.tensor_scalar(var2[:, tiles_of(g, 0, nt)], mv[:, 0:nt, 1], EPS, None, ALU.add).then_inc(var2_ready, 1)

            def invert2(g, nt):
                dve.wait_ge(std2_ready, g + 1)
                nc.vector.reciprocal(rstd2[:, tiles_of(g, 0, nt)], std2[:, tiles_of(g, 0, nt)]).then_inc(rstd2_ready, 1)

            def route_bits(g, nt):
                dve.wait_ge(score_done, g + 1)
                nc.vector.tensor_scalar(bitsT[:, 0:nt * R], side[:, 0:nt * R], cols_sb[:, 2 * PAIRS:2 * PAIRS + 1], 0.0,
                                        ALU.add, ALU.is_ge).then_inc(bits_ready, 1)

            def route(g, nt):
                at = 2 * PAIRS + 1
                dve.wait_ge(count_done, 2 * g + 1)
                nc.vector.tensor_scalar(routeT[:, 0:nt * R], ring[1][:, 0:nt * R], cols_sb[:, at:at + 1],
                                        cols_sb[:, at + 2:at + 3], ALU.is_ge, ALU.mult).then_inc(route_ready, 1)
                dve.wait_ge(count_done, 2 * g + 2)
                nc.vector.tensor_scalar(selT[:, 0:nt * R], side[:, 0:nt * R], cols_sb[:, at + 1:at + 2],
                                        None, ALU.is_ge).then_inc(route_ready, 1)

            x_split_lo(0, 0)
            split_lo(0)
            split_lo(1)
            x_split_lo(0, 1)
            for i in (2, 3):
                split_lo(i)
            dve.wait_ge(consts, 16 * CONSTS)
            nc.vector.tensor_tensor(pos_sb[:, :], pos_sb[:, :], xn[:, 0, :], ALU.add).then_inc(pos_ready, 1)
            dve.wait_ge(pos_ready, 1)
            for tp in range(2):
                embed(0, GT, tp)
                half_moments(0, tp)
            moments(0, GT)
            normalise(0, GT)
            split_lo(4)
            transposed_lo(0, GT)
            split_lo(5)
            split_lo(6)
            dve.wait_ge(consts2, 16 * CONSTS2)
            for tp in range(2):
                v_evac(0, GT, 0, tp)
            q_evac_lo(0, GT, 0)
            k_evac_lo(0, GT, 0)

            def attention(g, nt, nxt):
                for j in range(1, PAIRS + 2):
                    if j < PAIRS:
                        if j % 2 == 0:
                            for tp in range(nt // 2):
                                v_evac(g, nt, j // 2, tp)
                        if j == 5 and nxt:
                            if first_group(g):
                                dve.wait_ge(piece_lo, P1_PIECES - 2)
                            else:
                                dve.wait_ge(bias_rows, 16 * 3)
                            for tp in range(nxt // 2):
                                embed(g + 1, nxt, tp)
                        q_evac_lo(g, nt, j)
                        k_evac_lo(g, nt, j)
                    if j == 8:
                        transposed_lo(g + 1, nxt or GT)
                    if j == 2 and not first_group(g):
                        residual(g - 1, GT)
                    if j == 4 and nt == GT and not first_group(g):
                        moments2(g - 1, GT)
                    if j == 6 and nxt:
                        moments(g + 1, nxt)
                    if j == 7 and nxt:
                        normalise(g + 1, nxt)
                    if j < PAIRS + 1:
                        s_evac(g, nt, j - 1)
                    for i in late_pieces(g, j):
                        split_lo(i)
                    if j == PAIRS + 1 and nxt:
                        for tp in range(nxt // 2):
                            v_evac(g + 1, nxt, 0, tp)
                    elif j == PAIRS + 1:
                        route_bits(0, GT)
                    if j >= 2:
                        o_evac_lo(g, nt, j - 2)
                    if j == PAIRS + 1 and nxt:
                        q_evac_lo(g + 1, nxt, 0)
                        k_evac_lo(g + 1, nxt, 0)
                    if j == 8 and nt < GT:
                        moments2(g - 1, GT)
                    if j == (6 if nt == GT else 9) and not first_group(g):
                        invert2(g - 1, GT)

            for_groups(dve, attention)
            route(0, GT)
            residual(GROUPS - 1, TAIL)
            moments2(GROUPS - 1, TAIL)
            invert2(GROUPS - 1, TAIL)

            def mask_hidden(g, nt, s):
                q, c = divmod(s - QUAD, QUAD)
                turns = len(range(q % PLACES, QUADS, PLACES))
                dve.wait_ge(up_done, 3 * CH * g + s + 1)
                if c == 0:
                    dve.wait_ge(spread[q % PLACES], 16 * QUAD * (turns * g + q // PLACES + 1))
                h = hid_ps[s % 3][:, 0:nt * R]
                at = 2 * PAIRS + 4 + s
                nc.vector.scalar_tensor_tensor(h, h, cols_sb[:, at:at + 1], masks[q % PLACES][:, c, 0:nt * R],
                                               ALU.add, ALU.subtract).then_inc(masked, 1)

            def hidden_lo(g, nt, s):
                dve.wait_ge(hid_hi, 3 * CH * g + s + 1)
                nc.vector.scalar_tensor_tensor(pairT[:, s % 3, 1, 0:nt * R], hid_ps[s % 3][:, 0:nt * R], 0.0,
                                               pairT[:, s % 3, 0, 0:nt * R].bitcast(f32), ALU.max, ALU.subtract).then_inc(hid_lo, 1)

            def softmax_in(g, nt):
                dve.wait_ge(att_done, g + 1)
                nc.vector.scalar_tensor_tensor(soft_in[:, 0:nt * R].rearrange("p (t r) -> p t r", r=R),
                                               ring[0][0:R, 0:nt * R].rearrange("p (t r) -> p t r", r=R), float(D) ** -0.5,
                                               maskb_sb[:, :].unsqueeze(1).to_broadcast([R, nt, R]),
                                               ALU.mult, ALU.add).then_inc(soft_step, 1)
                dve.wait_ge(soft_step, 3 * g + 1)
                nc.vector.tensor_reduce(row_inv[:, 0:nt], soft_in[:, 0:nt * R].rearrange("p (t r) -> p t r", r=R),
                                        AX.X, ALU.max).then_inc(soft_step, 1)
                dve.wait_ge(soft_step, 3 * g + 2)
                nc.vector.tensor_scalar(neg_max[:, 0:nt], row_inv[:, 0:nt], -1.0, None, ALU.mult).then_inc(max_ready, 1)

            def finish(g, nt):
                dve.wait_ge(exp_ready, g + 1)
                nc.vector.reciprocal(row_inv[:, 0:nt], row_sum[:, 0:nt]).then_inc(soft_step, 1)
                dve.wait_ge(soft_step, 3 * g + 3)
                if not first_group(g):
                    dve.wait_ge(stored, 16 * g)
                for tp in range(nt // 2):
                    dve.wait_ge(av_done, 2 * g + tp + 1)
                    for t in (2 * tp, 2 * tp + 1):
                        last = nc.vector.scalar_tensor_tensor(out_sb[:, t, :], ring[tp][0:R, t % 2 * D:(t % 2 + 1) * D],
                                                              row_inv[:, t:t + 1],
                                                              h_all[0:R, tiles_of(g, t, 1), :].rearrange("p t n -> p (t n)"),
                                                              ALU.mult, ALU.add)
                    last.then_inc(out_ready, 1)

            def ffn(g, nt, nxt, first=False):
                for s in range(TREES * CH + 2):
                    if QUAD <= s < TREES * CH:
                        mask_hidden(g, nt, s)
                    if 1 <= s <= TREES * CH:
                        hidden_lo(g, nt, s - 1)
                    if s == 1 and not first:
                        softmax_in(g - 1, GT)
                    if s == 7 and not first:
                        finish(g - 1, GT)
                    if not nxt and s == 2 * CH + 4:
                        softmax_in(g, nt)
                    if s == TREES * CH and nxt:
                        transposed_lo(GROUPS + g + 1, nxt)
                dve.wait_ge(down_done, 3 * CH * (g + 1))
                for tp in range(nt // 2):
                    last = nc.vector.tensor_copy(v2[:, 2 * tp:2 * tp + 2, :], down[tp][0:R, :].rearrange("p (t n) -> p t n", t=2))
                last.then_inc(down_v, 1)
                if nxt:
                    route_bits(g + 1, nxt)
                    route(g + 1, nxt)

            ffn(0, GT, GT, first=True)
            with dve.Fori(1, GROUPS - 2) as g:
                ffn(g, GT, GT)
            ffn(GROUPS - 2, GT, TAIL)
            ffn(GROUPS - 1, TAIL, 0)
            finish(GROUPS - 1, TAIL)

        @block.tensor
        def _(pe):
            def embed(g, nt):
                for t in range(nt):
                    if t % 2 == 0:
                        pe.wait_ge(x_lo, 2 * g + t // 2 + 1)
                    for k in range(KX):
                        if first_group(g) and t == 0 and k * D % STAGE == 0:
                            pe.wait_ge(piece_lo, k * D // STAGE + 1)
                        for n, (a, b) in enumerate(PRODUCTS):
                            at = (XLO if a else XHI) + t * KX * R + k * R
                            last = nc.tensor.matmul(embed_bank(nt, t // 2)[0:R, t % 2 * D:(t % 2 + 1) * D], arena[:, at:at + R],
                                                    tok_w(k, b), start=(k == n == 0), stop=(k == KX - 1 and n == 2),
                                                    skip_group_check=True)
                    if t % 2:
                        last.then_inc(tok_done, 1)

            def turn(n, nt):
                pe.wait_ge(xn_ready, n + 1)
                for k in range(KD):
                    for t in range(nt):
                        last = nc.tensor.transpose(ring[k][:, t * R:(t + 1) * R], xn[:, t, k * 128:(k + 1) * 128],
                                                   id_sb[0:R, 0:R])
                    last.then_inc(t_done, 1)

            def values(g, nt, quarter, tp):
                bank = v_bank(nt, quarter, tp)
                if quarter == 0:
                    pe.wait_ge(xT_lo, KD * (g + 1))
                elif nt == GT:
                    pe.wait_ge(k_ready if tp else q_ready, PAIRS * g + 2 * quarter)
                elif quarter == 1:
                    pe.wait_ge(q_ready, PAIRS * g + 2)
                else:
                    pe.wait_ge(v_ready, PAIRS * g + quarter)
                for t in (2 * tp, 2 * tp + 1):
                    n = 0
                    for k in range(KD):
                        for a, b in PRODUCTS:
                            last = nc.tensor.matmul(bank[0:R, t % 2 * D:(t % 2 + 1) * D],
                                                    xT[:, a, k, t * R:(t + 1) * R], in_w(WV, k, quarter * D, D, b),
                                                    start=(n == 0), stop=(n == 5), skip_group_check=True)
                            n += 1
                last.then_inc(v_done, 1)

            def project(nt, j, which, base, done):
                bank = qk_banks(nt, j)[which]
                n = 0
                for k in range(KD):
                    for a, b in PRODUCTS:
                        last = nc.tensor.matmul(bank[:, 0:nt * R], in_w(base, k, 128 * j, 128, a),
                                                xT[:, b, k, 0:nt * R], start=(n == 0), stop=(n == 5))
                        n += 1
                last.then_inc(done, 1)

            def scores(g, nt, j):
                pe.wait_ge(q_ready, PAIRS * g + j + 1)
                pe.wait_ge(k_ready, PAIRS * g + j + 1)
                for t in range(nt):
                    if t % 2 == 0:
                        if j:
                            pe.wait_ge(s_ready, 2 * PAIRS * g + nt // 2 * (j - 1) + t // 2 + 1)
                    for n, (a, b) in enumerate(PRODUCTS):
                        last = nc.tensor.matmul(s_ps[t // 2][0:R, t % 2 * 2 * R:(t % 2 + 1) * 2 * R],
                                                (k_low if a else k_high)[:, j % 2, t * R:(t + 1) * R],
                                                q_pad[:, b, j % 2, t, :, :].rearrange("p h r -> p (h r)"),
                                                start=(n == 0), stop=(n == 2), skip_group_check=True)
                    if t % 2:
                        last.then_inc(s_done, 1)

            def mix(g, nt, j):
                pe.wait_ge(v_ready, PAIRS * g + nt // 2 * (j // 2 + 1))
                for t in range(nt):
                    if t % 2 == 0:
                        pe.wait_ge(s_ready, 2 * PAIRS * g + nt // 2 * j + t // 2 + 1)
                        if j:
                            pe.wait_ge(o_lo, 2 * PAIRS * g + nt // 2 * (j - 1) + t // 2 + 1)
                    last = nc.tensor.matmul(o_ps[t // 2][:, t % 2 * 2 * R:(t % 2 + 1) * 2 * R],
                                            v_sb[0:R, j // 2 % 2, t, j % 2 * 128:(j % 2 + 1) * 128],
                                            s_sb[0:R, j % 2, t, :], start=True, stop=True, skip_group_check=True)
                    if t % 2:
                        last.then_inc(o_done, 1)

            def project_out(g, nt, j):
                pe.wait_ge(o_lo, 2 * PAIRS * g + nt // 2 * (j + 1))
                if j == 0 and not first_group(g):
                    pe.wait_ge(h2_ready, 2 * g)
                for t in range(nt):
                    for n, (a, b) in enumerate(PRODUCTS):
                        last = nc.tensor.matmul(wo_acc[t // 2][0:R, t % 2 * D:(t % 2 + 1) * D],
                                                pairT[:, j % 2, a, t * R:(t + 1) * R], out_w(WO, j, 0, D, b),
                                                start=(j == 0 and n == 0 and t % 2 == 0),
                                                stop=(j == PAIRS - 1 and n == 2), skip_group_check=True)
                last.then_inc(wo_done, 1)

            def node_scores(g, nt):
                if first_group(g):
                    pe.wait_ge(piece_lo, P1_PIECES)
                pe.wait_ge(xT_lo, KD * (GROUPS + g + 1))
                n = 0
                for k in range(KD):
                    for a, b in PRODUCTS:
                        last = nc.tensor.matmul(side[:, 0:nt * R], node_w[:, a, k, :], xT[:, b, k, 0:nt * R],
                                                start=(n == 0), stop=(n == 5))
                        n += 1
                last.then_inc(score_done, 1)

            def path_counts(g, nt):
                pe.wait_ge(bits_ready, g + 1)
                nc.tensor.matmul(ring[1][:, 0:nt * R], steer_sb[:, 0:128], bitsT[:, 0:nt * R],
                                 start=True, stop=True).then_inc(count_done, 1)
                nc.tensor.matmul(side[:, 0:nt * R], steer_sb[:, 128:256], bitsT[:, 0:nt * R],
                                 start=True, stop=True).then_inc(count_done, 1)

            embed(0, GT)
            pe.wait_ge(consts, 16 * CONSTS)
            turn(0, GT)
            pe.wait_ge(prelude, 1)

            pe.wait_ge(piece_lo, WT_PIECES + 1)
            for tp in range(2):
                values(0, GT, 0, tp)
            pe.wait_ge(piece_lo, WT_PIECES + 2)
            project(GT, 0, 0, WQ, q_done)
            pe.wait_ge(piece_lo, WT_PIECES + 3)
            project(GT, 0, 1, WK, k_done)

            def attention(g, nt, nxt):
                for j in range(1, PAIRS + 2):
                    if first_group(g) and j == PAIRS // 2:
                        pe.wait_ge(piece_lo, WT_PIECES + HALF_PIECES + 1)
                    if first_group(g) and j in (3, 3 + PAIRS // 2):
                        pe.wait_ge(piece_lo, WT_PIECES + (HALF_PIECES if j > 3 else 0) + 4)
                    if j < PAIRS:
                        if j % 2 == 0:
                            for tp in range(nt // 2):
                                values(g, nt, j // 2, tp)
                        if j == 5 and nxt:
                            pe.wait_ge(q_ready, PAIRS * g + j)
                            pe.wait_ge(k_ready, PAIRS * g + j)
                            embed(g + 1, nxt)
                        if nt < GT:
                            if j == 3:
                                pe.wait_ge(v_ready, PAIRS * g + 2)
                            elif j > 3:
                                pe.wait_ge(q_ready, PAIRS * g + j - 1)
                        elif j < 2 or j % 2 == 0:
                            pe.wait_ge(v_ready, PAIRS * g + j // 2 * 2 + 1)
                        elif j == 5 and nxt == GT:
                            pe.wait_ge(h_ready, 2 * (g + 1) + 1)
                        else:
                            pe.wait_ge(q_ready, PAIRS * g + j)
                        if first_group(g) and j == PAIRS // 2:
                            pe.wait_ge(piece_lo, WT_PIECES + HALF_PIECES + 2)
                        project(nt, j, 0, WQ, q_done)
                        if j == 1 and not first_group(g):
                            project_out(g - 1, GT, PAIRS - 1)
                        if nt < GT:
                            if j == 1:
                                pe.wait_ge(v_ready, PAIRS * g + 1)
                            else:
                                pe.wait_ge(k_ready, PAIRS * g + j - 1)
                        elif j < 2 or j % 2 == 0:
                            pe.wait_ge(v_ready, PAIRS * g + j // 2 * 2 + 2)
                        elif j == 5 and nxt:
                            pe.wait_ge(h_ready, 2 * (g + 1) + nxt // 2)
                        else:
                            pe.wait_ge(k_ready, PAIRS * g + j)
                        if first_group(g) and j == PAIRS // 2:
                            pe.wait_ge(piece_lo, WT_PIECES + HALF_PIECES + 3)
                        project(nt, j, 1, WK, k_done)
                    if j == 8:
                        pe.wait_ge(q_ready, PAIRS * (g + 1))
                        pe.wait_ge(k_ready, PAIRS * (g + 1))
                        turn(g + 1, nxt or GT)
                    if j < PAIRS + 1:
                        scores(g, nt, j - 1)
                    if j == PAIRS + 1 and nxt:
                        for tp in range(nxt // 2):
                            values(g + 1, nxt, 0, tp)
                    elif j == PAIRS + 1:
                        node_scores(0, GT)
                    if j >= 2:
                        mix(g, nt, j - 2)
                    if j == PAIRS + 1 and nxt:
                        project(nxt, 0, 0, WQ, q_done)
                    if j >= 3:
                        project_out(g, nt, j - 3)
                    if j == PAIRS + 1 and nxt:
                        project(nxt, 0, 1, WK, k_done)

            for_groups(pe, attention)
            path_counts(0, GT)
            project_out(GROUPS - 1, TAIL, PAIRS - 1)

            def up(g, nt, s):
                tree, c = s // CH, s % CH
                if s >= 3:
                    pe.wait_ge(hid_lo, 3 * CH * g + s - 2)
                elif not first_group(g):
                    pe.wait_ge(hid_lo, 3 * CH * g)
                n = 0
                for k in range(KD):
                    for a, b in PRODUCTS:
                        last = nc.tensor.matmul(hid_ps[s % 3][:, 0:nt * R], in_w(W1[tree], k, 128 * c, 128, a),
                                                xT[:, b, k, 0:nt * R], start=(n == 0), stop=(n == 5 and s >= QUAD))
                        n += 1
                if s == 0:
                    pe.wait_ge(route_ready, 2 * g + 2)
                if s < QUAD:
                    last = nc.tensor.matmul(hid_ps[s % 3][:, 0:nt * R], e_sb[:, 128 * c:128 * (c + 1)], routeT[:, 0:nt * R],
                                            start=False, stop=True)
                last.then_inc(up_done, 1)

            def down_step(g, nt, s):
                tree, c = s // CH, s % CH
                pe.wait_ge(hid_lo, 3 * CH * g + s + 1)
                if c == 0 and tree:
                    pe.wait_ge(down_q, 2 * g + tree)
                elif c == 0 and not first_group(g):
                    pe.wait_ge(down_v, g)
                if tree < 2:
                    for m in range(KD):
                        for n, (a, b) in enumerate(PRODUCTS):
                            last = nc.tensor.matmul(down[m][:, 0:nt * R], out_w(W2[tree], c, 128 * m, 128, a),
                                                    pairT[:, s % 3, b, 0:nt * R], start=(c == n == 0), stop=False,
                                                    skip_group_check=True)
                        if c == CH - 1:
                            last = nc.tensor.matmul(down[m][:, 0:nt * R], b2_sb[:, tree, 128 * m:128 * (m + 1)],
                                                    selT[:, 0:nt * R], start=False, stop=True, skip_group_check=True)
                else:
                    for t in range(nt):
                        acc = down[t // 2][0:R, t % 2 * D:(t % 2 + 1) * D]
                        for n, (a, b) in enumerate(PRODUCTS):
                            last = nc.tensor.matmul(acc, pairT[:, s % 3, a, t * R:(t + 1) * R], out_w(W2[tree], c, 0, D, b),
                                                    start=(c == n == 0 and t % 2 == 0), stop=False, skip_group_check=True)
                        if c == CH - 1:
                            last = nc.tensor.matmul(acc, selT[:, t * R:(t + 1) * R], b2_sb[:, tree, :],
                                                    start=False, stop=True, skip_group_check=True)
                last.then_inc(down_done, 1)

            def attend(g, nt):
                pe.wait_ge(down_q, 2 * (g + 1))
                for t in range(nt):
                    for k in range(KD):
                        last = nc.tensor.matmul(ring[0][0:R, t * R:(t + 1) * R], qT[:, 0, k, t * R:(t + 1) * R],
                                                qT[:, 1, k, t * R:(t + 1) * R], start=(k == 0), stop=(k == KD - 1),
                                                skip_group_check=True)
                last.then_inc(att_done, 1)

            def turn_probs(g, nt):
                pe.wait_ge(exp_ready, g + 1)
                for t in range(nt):
                    last = nc.tensor.transpose(ring[1][0:R, t * R:(t + 1) * R], probs[:, t * R:(t + 1) * R], id_sb[0:R, 0:R])
                last.then_inc(pt_done, 1)

            def weigh(g, nt):
                pe.wait_ge(pt_ready, g + 1)
                pe.wait_ge(down_v, g + 1)
                for t in range(nt):
                    last = nc.tensor.matmul(ring[t // 2][0:R, t % 2 * D:(t % 2 + 1) * D], probsT[:, t * R:(t + 1) * R],
                                            v2[:, t, :], start=True, stop=True, skip_group_check=True)
                    if t % 2:
                        last.then_inc(av_done, 1)

            pe.wait_ge(bias_rows, 16 * 3)

            def ffn(g, nt, nxt, first=False):
                for s in range(TREES * CH + 2):
                    if first and s % CH == 0 and s < TREES * CH:
                        pe.wait_ge(piece_lo, P1_PIECES + (s // CH) * 4 + 2)
                    if first and s % CH == 2 and s < TREES * CH:
                        pe.wait_ge(piece_lo, P1_PIECES + (s // CH) * 4 + 4)
                    if first and s == 2:
                        pe.wait_ge(h2_ready, 2 * (GROUPS - 1) + TAIL // 2)
                    if s < TREES * CH:
                        up(g, nt, s)
                    if s == 5 and not first:
                        pe.wait_ge(route_ready, 2 * g + 2)
                        turn_probs(g - 1, GT)
                    if s == 7 and not first:
                        weigh(g - 1, GT)
                    if s == TREES * CH and nxt:
                        if not first:
                            pe.wait_ge(out_ready, 2 * g)
                        turn(GROUPS + g + 1, nxt)
                    if not nxt and s == 2 * CH + 3:
                        pe.wait_ge(out_ready, 2 * g)
                        attend(g, nt)
                    if not nxt and s == TREES * CH:
                        turn_probs(g, nt)
                    if s >= 2:
                        down_step(g, nt, s - 2)
                if nxt:
                    node_scores(g + 1, nxt)
                    attend(g, nt)
                    path_counts(g + 1, nxt)

            ffn(0, GT, GT, first=True)
            with pe.Fori(1, GROUPS - 2) as g:
                ffn(g, GT, GT)
            ffn(GROUPS - 2, GT, TAIL)
            ffn(GROUPS - 1, TAIL, 0)
            weigh(GROUPS - 1, TAIL)


def launch_arrays(i):
    f = np.float32
    x = np.zeros((TILES * PER_TILE,) + i["x"].shape[1:], f)
    x[:IMAGES] = i["x"]
    n = SIDE // PATCH
    x = x.reshape(TILES, PER_TILE, CHANNELS, n, PATCH, n, PATCH).transpose(0, 2, 4, 6, 1, 3, 5)
    x = x.reshape(TILES, KX, 128, PER_TILE * PATCHES).transpose(0, 2, 1, 3)
    xt = np.zeros((TILES, 128, KX, ROWS), f)
    xt[..., :PER_TILE * PATCHES] = x

    def chunks(w):
        return w.reshape(-1, 128, w.shape[1]).transpose(1, 0, 2).reshape(128, -1)

    def by_halves(w):
        return w.reshape(KD, 128, 2, 512).transpose(1, 2, 0, 3).reshape(128, -1)

    def padded(w, rows):
        return np.concatenate([w, np.zeros((rows - w.shape[0],) + w.shape[1:], w.dtype)])

    trees = "qkv"
    node_w = np.concatenate([padded(i[f"L0_ffn_{t}_node_w"], LEAVES) for t in trees])
    mats = {WT: chunks(i["L0_tok_W"].T), NODE_W: chunks(padded(node_w, 128).T)}
    attn = {WQ: by_halves(i["L0_attn_Wq"]), WK: by_halves(i["L0_attn_Wk"]), WV: by_halves(i["L0_attn_Wv"]),
            WO: chunks(i["L0_attn_Wo"])}
    ffn = {}
    for t, c in enumerate(trees):
        ffn[W1[t]] = by_halves(i[f"L0_ffn_{c}_w1"].transpose(1, 0, 2).reshape(D, HID))
        ffn[W2[t]] = chunks(i[f"L0_ffn_{c}_w2"].reshape(HID, D))
    weights = np.concatenate([(mats | (attn if n < P1_PIECES else ffn))[dst][:, off:off + width]
                              for n, (_, width, dst, _, off) in enumerate(PIECES)], 1)

    patch_rows, real = PER_TILE * PATCHES, PER_TILE * (PATCHES + 1)
    p = i["L0_tok_pos_embedding"][0]
    pos = np.zeros((2, ROWS, D), f)
    pos[0, :patch_rows] = np.tile(p[1:], (PER_TILE, 1))
    pos[0, patch_rows:real] = p[0]
    pos[1, :patch_rows] = i["L0_tok_b"]
    pos[1, patch_rows:real] = i["L0_tok_cls_token"][0, 0]
    image = np.concatenate([np.arange(patch_rows) // PATCHES, np.arange(ROWS - patch_rows)])
    same = image[:, None] == image[None, :]

    node_b = np.full((128,), -1.0, f)
    for t, c in enumerate(trees):
        node_b[LEAVES * t:LEAVES * t + NODES] = i[f"L0_ffn_{c}_node_b"]
    steer = np.zeros((128, 2, 128), f)
    thr = np.ones((2, 128), f)
    thr[0, ONE_ROW:ONE_ROW + 3] = 0.0
    value = np.full((128,), BIG, f)
    value[ONE_ROW:ONE_ROW + 3] = 1.0
    e_mask = np.zeros((128, TREES, LEAVES, LEAF_W), f)
    for t in range(TREES):
        for leaf in range(LEAVES):
            off, sel = OFF_ROW + LEAVES * t + leaf, [row + LEAVES * t + leaf for row in SEL_ROWS]
            node, rights = leaf + NODES, 0
            while node:
                parent = (node - 1) // 2
                right = node == 2 * parent + 2
                rights += right
                steer[LEAVES * t + parent, 1, sel] = 1.0 if right else -1.0
                node = parent
            steer[:, 0, off] = -steer[:, 1, sel[0]]
            thr[1, sel], thr[0, off] = rights, 1 - rights
            e_mask[off, t, leaf] = -1.0
    cols = np.stack([*i["L0_attn_bq"].reshape(PAIRS, 128), *i["L0_attn_bk"].reshape(PAIRS, 128), node_b, *thr, value,
                     *np.concatenate([i[f"L0_ffn_{c}_b1"].reshape(CH, 128) for c in trees])], 1)
    b2 = np.zeros((128, TREES, D), f)
    for t, c in enumerate(trees):
        for row in SEL_ROWS:
            b2[row + LEAVES * t:row + LEAVES * (t + 1), t] = i[f"L0_ffn_{c}_b2"]
    bf = mybir.dt.np(mybir.dt.bfloat16)
    return dict(
        x=xt.reshape(TILES, 128, -1), weights=weights, pos=pos[0], tok=pos[1], ident=np.eye(128, dtype=f),
        mask=np.where(same, f(HD ** -0.5), f(0)), mask_bias=np.where(same, f(0), f(-1e30)),
        bv=np.tile(i["L0_attn_bv"], (ROWS, 1)), bo=np.tile(i["L0_attn_bo"], (ROWS, 1)), cols=cols.astype(f),
        e_mask=e_mask.reshape(128, -1)[:, :QUAD * 128].astype(bf), b1=i["L0_ffn_q_b1"].reshape(1, -1)[:, :QUAD * 128],
        b2=b2.reshape(128, -1), steer=steer.reshape(128, -1).astype(bf))


def kernel(**inputs):
    import concourse.bacc as bacc
    from concourse.bass_utils import run_bass_kernel_spmd

    arrays = {k: np.ascontiguousarray(v) for k, v in launch_arrays({k: np.asarray(v) for k, v in inputs.items()}).items()}
    nc = bacc.Bacc("TRN2", target_bir_lowering=False, num_devices=1)
    args = {k: nc.dram_tensor(k, a.shape, mybir.dt.from_np(a.dtype), kind="ExternalInput").ap() for k, a in arrays.items()}
    out = nc.dram_tensor("out", (TILES, ROWS, D), mybir.dt.float32, kind="ExternalOutput").ap()
    build_program(nc, *args.values(), out)
    got = run_bass_kernel_spmd(nc, [arrays], core_ids=[0]).results[0]["out"]
    patch_rows, real = PER_TILE * PATCHES, PER_TILE * (PATCHES + 1)
    patches = got[:, :patch_rows].reshape(TILES * PER_TILE, PATCHES, D)
    return np.concatenate([got[:, patch_rows:real].reshape(TILES * PER_TILE, 1, D), patches], 1)[:IMAGES]
```
